# Optimizing a Trainium2 kernel written in Bass

```python
import numpy as np
import jax
import jax.numpy as jnp

def _softmax(x, axis=-1):
    return jax.nn.softmax(x, axis=axis)

def _gelu(x):
    return jax.nn.gelu(x, approximate=True)

def _silu(x):
    return jax.nn.silu(x)

def _sigmoid(x):
    return jax.nn.sigmoid(x)

def _layernorm(x, axis=-1, eps=1e-05):
    m = jnp.mean(x, axis=axis, keepdims=True)
    v = jnp.var(x, axis=axis, keepdims=True)
    return (x - m) / jnp.sqrt(v + eps)

def _scatter_add(tgt, idx, src, axis=0):
    return tgt.at[idx].add(src)

def _segment_sum(src, seg, n):
    return jax.ops.segment_sum(src, seg, n)
kernel_name = 'mk_adj_ffn_d1_adj_r2_de0d4d'

def setup_inputs(seed: int=0):
    np.random.seed(seed)
    _w = jnp.asarray

    def _rec_inputs():
        import jax
        import jax.numpy as jnp
        _gk = jax.random.key(seed)
        x = -0.0005207 + 1.001 * jax.random.normal(jax.random.fold_in(_gk, 1), (4096, 128), jnp.float32)
        _a = jax.random.bernoulli(jax.random.fold_in(_gk, 2), 0.000488281, (4096, 4096))
        _a = jnp.logical_or(_a, jnp.swapaxes(_a, -1, -2))
        _a = jnp.logical_or(_a, jnp.eye(4096, dtype=bool))
        _af = _a.astype(jnp.float32)
        _af = _af * jax.random.uniform(jax.random.fold_in(_gk, 3), (4096, 4096), jnp.float32, 0.05, 1)
        adj = _af
        return (x, adj)
    x, adj = _rec_inputs()

    def _L0_gnn_setup():
        import jax, jax.numpy as jnp
        import numpy as np
        N, F, OUT = (4096, 128, 128)
        key = jax.random.key(seed)
        k1, k2, k3, k4 = jax.random.split(key, 4)
        features = jax.random.normal(k1, (N, F), dtype=jnp.float32)
        adj = jax.random.uniform(k2, (N, N), dtype=jnp.float32)
        gain = float(np.sqrt(2.0))
        b_n = gain * np.sqrt(6.0 / (F + F))
        neigh_W = jax.random.uniform(k3, (F, F), dtype=jnp.float32, minval=-b_n, maxval=b_n)
        b_l = gain * np.sqrt(6.0 / (2 * F + OUT))
        lin_W = jax.random.uniform(k4, (OUT, 2 * F), dtype=jnp.float32, minval=-b_l, maxval=b_l)
        return {'features': features, 'adj': adj, 'neigh_W': neigh_W, 'lin_W': lin_W}
    _L0_gnn_all = _L0_gnn_setup()
    _L0_gnn_in = {k: v for k, v in _L0_gnn_all.items() if k in ('neigh_W', 'lin_W')}
    del _L0_gnn_all

    def _L0_ffn_setup():
        import jax, jax.numpy as jnp
        import numpy as np
        B, T, C = (64, 192, 128)
        NH, NKV = (4, 2)
        HD = C // NH
        NREP = NH // NKV
        NE, TOPK = (8, 2)
        HID = int(8 / 3 * C)
        EPS_RMS = 1e-06

        def _rope_tables(t_len):
            inv_freq = 1.0 / 10000.0 ** (np.arange(0, HD, 2, dtype=np.float32) / HD)
            t = np.arange(t_len, dtype=np.float32)
            freqs = np.outer(t, inv_freq)
            emb = np.concatenate([freqs, freqs], axis=-1)
            return (jnp.asarray(np.cos(emb)), jnp.asarray(np.sin(emb)))

        def _rotate_half(x):
            h = x.shape[-1] // 2
            return jnp.concatenate([-x[..., h:], x[..., :h]], axis=-1)

        def _rmsnorm(v, w):
            return v * jax.lax.rsqrt(jnp.mean(v * v, axis=-1, keepdims=True) + EPS_RMS) * w
        key = jax.random.key(seed)
        ks = jax.random.split(key, 10)
        s = lambda k, shape: jax.random.normal(k, shape, jnp.float32) * 0.02
        return {'x': jax.random.normal(ks[0], (B, T, C), jnp.float32), 'ln1_w': jnp.ones((C,), jnp.float32), 'ln2_w': jnp.ones((C,), jnp.float32), 'wq': s(ks[1], (NH * HD, C)), 'wk': s(ks[2], (NKV * HD, C)), 'wv': s(ks[3], (NKV * HD, C)), 'wo': s(ks[4], (C, C)), 'router_w': s(ks[5], (NE, C)), 'w1': s(ks[6], (NE, HID, C)), 'w2': s(ks[7], (NE, C, HID)), 'w3': s(ks[8], (NE, HID, C))}
    _L0_ffn_all = _L0_ffn_setup()
    _L0_ffn_in = {k: v for k, v in _L0_ffn_all.items() if k in ('ln1_w', 'ln2_w', 'wq', 'wk', 'wv', 'wo', 'router_w', 'w1', 'w2', 'w3')}
    del _L0_ffn_all
    return {'x': x, 'adj': adj, 'L0_gnn_neigh_W': _L0_gnn_in['neigh_W'], 'L0_gnn_lin_W': _L0_gnn_in['lin_W'], 'L0_ffn_ln1_w': _L0_ffn_in['ln1_w'], 'L0_ffn_ln2_w': _L0_ffn_in['ln2_w'], 'L0_ffn_wq': _L0_ffn_in['wq'], 'L0_ffn_wk': _L0_ffn_in['wk'], 'L0_ffn_wv': _L0_ffn_in['wv'], 'L0_ffn_wo': _L0_ffn_in['wo'], 'L0_ffn_router_w': _L0_ffn_in['router_w'], 'L0_ffn_w1': _L0_ffn_in['w1'], 'L0_ffn_w2': _L0_ffn_in['w2'], 'L0_ffn_w3': _L0_ffn_in['w3']}

def reference(x, adj, L0_gnn_neigh_W, L0_gnn_lin_W, L0_ffn_ln1_w, L0_ffn_ln2_w, L0_ffn_wq, L0_ffn_wk, L0_ffn_wv, L0_ffn_wo, L0_ffn_router_w, L0_ffn_w1, L0_ffn_w2, L0_ffn_w3):
    import jax
    import jax.numpy as jnp

    def _L0_gnn_ref(features, adj, neigh_W, lin_W):
        import jax, jax.numpy as jnp
        import numpy as np
        N, F, OUT = (4096, 128, 128)
        h = features @ neigh_W.T
        deg = adj.sum(axis=1, keepdims=True) + 1.0
        h = adj @ h / deg
        z = jnp.concatenate([features, h], axis=-1) @ lin_W.T
        return z

    def _L0_ffn_ref(x, ln1_w, ln2_w, wq, wk, wv, wo, router_w, w1, w2, w3):
        import jax, jax.numpy as jnp
        import numpy as np
        B, T, C = (64, 192, 128)
        NH, NKV = (4, 2)
        HD = C // NH
        NREP = NH // NKV
        NE, TOPK = (8, 2)
        HID = int(8 / 3 * C)
        EPS_RMS = 1e-06

        def _rope_tables(t_len):
            inv_freq = 1.0 / 10000.0 ** (np.arange(0, HD, 2, dtype=np.float32) / HD)
            t = np.arange(t_len, dtype=np.float32)
            freqs = np.outer(t, inv_freq)
            emb = np.concatenate([freqs, freqs], axis=-1)
            return (jnp.asarray(np.cos(emb)), jnp.asarray(np.sin(emb)))

        def _rotate_half(x):
            h = x.shape[-1] // 2
            return jnp.concatenate([-x[..., h:], x[..., :h]], axis=-1)

        def _rmsnorm(v, w):
            return v * jax.lax.rsqrt(jnp.mean(v * v, axis=-1, keepdims=True) + EPS_RMS) * w
        Bx, Tx, Cx = x.shape
        h = _rmsnorm(x, ln1_w)
        q = (h @ wq.T).reshape(Bx, Tx, NH, HD).transpose(0, 2, 1, 3)
        k = (h @ wk.T).reshape(Bx, Tx, NKV, HD).transpose(0, 2, 1, 3)
        v = (h @ wv.T).reshape(Bx, Tx, NKV, HD).transpose(0, 2, 1, 3)
        cos, sin = _rope_tables(Tx)
        cos, sin = (cos[None, None], sin[None, None])
        q = q * cos + _rotate_half(q) * sin
        k = k * cos + _rotate_half(k) * sin
        k = jnp.repeat(k, NREP, axis=1)
        v = jnp.repeat(v, NREP, axis=1)
        scores = jnp.einsum('bhtd,bhsd->bhts', q, k) / jnp.sqrt(jnp.float32(HD))
        causal = jnp.tril(jnp.ones((Tx, Tx), dtype=bool))
        scores = jnp.where(causal[None, None], scores, jnp.float32(-1e+30))
        att = jax.nn.softmax(scores, axis=-1)
        y = jnp.einsum('bhts,bhsd->bhtd', att, v).transpose(0, 2, 1, 3).reshape(Bx, Tx, Cx)
        x = x + y @ wo.T
        flat = _rmsnorm(x, ln2_w).reshape(-1, Cx)
        probs = jax.nn.softmax(flat @ router_w.T, axis=-1)
        tp, ti = jax.lax.top_k(probs, TOPK)
        tp = tp / (jnp.sum(tp, axis=-1, keepdims=True) + 1e-09)
        weights = jnp.sum(tp[..., None] * jax.nn.one_hot(ti, NE, dtype=flat.dtype), axis=1)
        out = jnp.zeros_like(flat)
        for e in range(NE):
            hh = jax.nn.silu(flat @ w1[e].T) * (flat @ w3[e].T)
            out = out + weights[:, e:e + 1] * (hh @ w2[e].T)
        return x + out.reshape(Bx, Tx, Cx)
    x = x + _L0_gnn_ref(_layernorm(x, axis=-1), adj, L0_gnn_neigh_W, L0_gnn_lin_W)
    x = x + _L0_ffn_ref(_layernorm(x, axis=-1)[None], L0_ffn_ln1_w, L0_ffn_ln2_w, L0_ffn_wq, L0_ffn_wk, L0_ffn_wv, L0_ffn_wo, L0_ffn_router_w, L0_ffn_w1, L0_ffn_w2, L0_ffn_w3)[0]
    return x

_drawn_inputs = setup_inputs


def setup_inputs(seed=0):
    import zlib

    import numpy as np

    out = dict(_drawn_inputs(seed))
    spreads = {'L0_ffn_ln1_w': (1.0, 0.6), 'L0_ffn_ln2_w': (1.0, 0.6)}
    factors = {'L0_ffn_wq': 8.0,
     'L0_ffn_wk': 8.0,
     'L0_ffn_wv': 8.0,
     'L0_ffn_wo': 8.0,
     'L0_ffn_router_w': 8.0,
     'L0_ffn_w1': 8.0,
     'L0_ffn_w2': 8.0,
     'L0_ffn_w3': 8.0}
    for name, (base, spread) in spreads.items():
        noise = np.random.default_rng([zlib.crc32(name.encode()), seed]).standard_normal(out[name].shape)
        drawn = base * np.exp(spread * noise) if base else spread * noise
        out[name] = jnp.asarray(drawn.astype(out[name].dtype))
    for name, factor in factors.items():
        out[name] = (out[name] * factor).astype(out[name].dtype)
    return out
```

```python
import concourse.bass as bass
from concourse import mybir
from concourse.alu_op_type import AluOpType as ALU
from contextlib import ExitStack
import numpy as np

fp32 = mybir.dt.float32
fp32r = mybir.dt.float32r
bf16 = mybir.dt.bfloat16
ACT = mybir.ActivationFunctionType
X_AXIS = mybir.AxisListType.X

P = 128
N = 4096
C = 128
TILES = N // P
CH = 512
NCH = N // CH
TPC = CH // P
NH, NKV, HD = 4, 2, 32
NE, HID = 8, 341
RING = 4
GRP = TPC
NGRP = TILES // GRP
POOL_GRPS = 6
POOL_ADDS = POOL_GRPS - 1
QS = 3
PB = 4
SCALE = 1.0 / float(np.sqrt(np.float32(HD)))
STACK = 3 * HD
MROW = STACK
KB = [(0, 128), (128, 128), (256, 85)]


def build(nc, x, adj_t, neigh_w, lin1_t, lin2_t, ln1, ln2, wq_t, wqr_t, wk_t, wv_t, wo_t,
          router_t, tri_in, w1_t, w3_t, w2_t, cos_t, sin_t, ident_in, mask_in, out):
    ctx = ExitStack()
    with ctx:
        def sb(name, shape, dt=fp32):
            return ctx.enter_context(nc.sbuf_tensor(name, shape, dt))

        def sem(name):
            return ctx.enter_context(nc.semaphore(name))

        xs = sb("xs", [P, TILES, C])
        us = sb("us", [P, TILES, C])
        hT = sb("hT", [P, N])
        kst = sb("kst", [P, NKV, N], fp32r)
        v1 = sb("v1", [P, TILES, NKV, 2 * HD])
        ident = sb("ident", [P, P])
        masks = sb("masks", [P, 2, P])
        maskb = sb("maskb", [P, 3, P], bf16)
        ln1s = sb("ln1s", [P, 1])
        ln2s = sb("ln2s", [P, 1])
        eps5 = sb("eps5", [P, 1])
        eps6 = sb("eps6", [P, 1])
        wqs = sb("wqs", [P, 2, P])
        wks = sb("wks", [P, P])
        wvs = sb("wvs", [P, NKV * HD])
        wos = sb("wos", [P, P])
        rts = sb("rts", [P, NE])
        ps = ctx.enter_context(nc.psum_tensor("ps", [P, 8, CH], fp32))

        gn = ExitStack()

        def gsb(name, shape, dt=fp32):
            return gn.enter_context(nc.sbuf_tensor(name, shape, dt))

        ring = gsb("ring", [P, RING, GRP, CH])
        gs = gsb("gs", [P, TILES, C])
        acc_p = gsb("acc_p", [P, GRP, CH])
        acc_v = gsb("acc_v", [P, GRP, CH])
        wn = gsb("wn", [P, P])
        w2l = gsb("w2l", [P, P])
        wg = gsb("wg", [P, 2, P])
        ones = gsb("ones", [P, P])
        cen = gsb("cen", [P, 2, TPC, C])
        nrm = gsb("nrm", [P, 2, TPC, C])
        sq = gsb("sq", [P, 2, TPC, C])
        xnT = gsb("xnT", [P, 2, CH])
        st = gsb("st", [P, 2, 8, TPC])
        deg = gsb("deg", [P, CH])
        rdeg = gsb("rdeg", [P, CH])
        aggT = gsb("aggT", [P, CH])

        s_x = [sem(f"x_loaded{c}") for c in range(2)]
        s_w = sem("gnn_weights_loaded")
        s_c = sem("constants_loaded")
        s_adj = [sem(f"adj_loaded{r}") for r in range(RING)]
        s_adj_pe = sem("adj_multiplied")
        s_adj_pool = sem("adj_summed_pool")
        s_adj_dve = sem("adj_summed_dve")
        s_one = sem("ones_set")
        s_wgp = sem("wg_product")
        s_wg = sem("wg_ready")
        s_cen = sem("x_centred")
        s_sq = sem("squares")
        s_var = sem("variance_sum")
        s_std = sem("deviation")
        s_lnst = sem("ln_steps")
        s_xn = sem("x_normalised")
        s_xt = sem("xn_transposed")
        s_xnT = sem("xnT_ready")
        s_gz = sem("gz_product")
        s_g = sem("g_ready")
        s_z = sem("z_added")
        s_fold = sem("degree_fold")
        s_deg = sem("degree_product")
        s_rdeg = sem("degree_steps")
        s_aggT = sem("aggregate_scaled")
        s_nat = sem("aggregate_transposed")
        s_x1 = sem("x1_steps")
        s_u = sem("u_ready")
        s_usq = sem("u_squares")
        s_ustd = sem("u_deviation")
        s_hn = sem("h_normalised")
        s_ht = sem("h_transposed")
        s_hT = sem("hT_ready")
        s_out = sem("out_stored")
        gn.close()
        qst = sb("qst", [P, QS, NH, CH], fp32r)
        pb = sb("pb", [P, PB, 2, CH])
        cs = sb("cs", [P, 2, 2, CH])
        hl = sb("hl", [P, 2, 2, CH], fp32r)
        mx = sb("mx", [P, NH * TPC, NCH])
        mred = sb("mred", [P, NH * TPC])
        mrow = sb("mrow", [NH * TPC, 2, P], fp32r)
        rec = sb("rec", [P, 2, CH])
        ta, tb = rec[:, 0, :], rec[:, 1, :]
        yT = sb("yT", [P, CH])
        sqa = sb("sqa", [P, TPC, C])
        sta = sb("sta", [P, 4, TPC])
        lg = sb("lg", [P, TILES, NE])
        pr = sb("pr", [P, TILES, NE])
        wt = sb("wt", [P, TILES, NE])
        rsm = sb("rsm", [P, 6, TILES])
        tri = sb("tri", [P, NE, NE])
        w1s = sb("w1s", [P, NE, HID])
        w3s = sb("w3s", [P, NE, HID])
        w2s = sb("w2s", [P, NE, len(KB), C])
        flat = pb[:, :, :, :].rearrange("p a b c -> p (a b c)")
        sil = flat[:, 0:2 * CH].rearrange("p (a c) -> p a c", c=CH)
        hh = flat[:, 2 * CH:8 * CH].rearrange("p (a k c) -> p a k c", a=2, c=CH)
        cmp = flat[:, 2 * CH:2 * CH + TILES * NE * NE].rearrange("p (n e j) -> p n e j", n=TILES, j=NE)
        eqs = cs[:, :, :, :].rearrange("p a b c -> p (a b c)").rearrange("p (n e j) -> p n e j", n=TILES, j=NE)

        s_cs = [sem(f"tables_loaded{b}") for b in range(2)]
        s_stk = [sem(f"stacks_filled{b}") for b in range(2)]
        s_m = [sem(f"maxima_placed{b}") for b in range(2)]
        s_moe = sem("expert_weights_loaded")
        s_mb = sem("masks_ready")
        s_fill = sem("ones_filled")
        s_item = sem("item_ready")
        s_free = sem("item_read")
        s_vec = sem("vector_steps")
        s_hl = sem("split_ready")
        s_mred = sem("maxima_reduced")
        s_qk = sem("scores_ready")
        s_exp = sem("probs_ready")
        s_pv = sem("values_added")
        s_y = sem("y_steps")
        s_ss = sem("attention_squares")
        s_sd = sem("attention_deviation")
        s_fn = sem("flat_normalised")
        s_rm = sem("router_shifted")
        s_re = sem("router_exp")
        s_ab = sem("up_products")
        s_sil = sem("silu_ready")
        s_hh = sem("hidden_ready")
        s_dn = sem("down_products")
        s_acc = sem("expert_added")

        def units_before(c):
            return sum(2 * TPC * (k + 1) for k in range(c))

        def items_of(c):
            found = []
            scores = [("max", c + 1, t, h, k) for t in range(TPC) for h in range(NH) for k in range(c + 2)]
            if c == -1:
                found += [(k, 0) for k in ("qa", "qb", "kk", "v")] + [(k, 1) for k in ("qa", "qb", "kk", "v")]
            if c + 1 < NCH:
                found += scores + [("mt", c + 1)]
            if c >= 1:
                post = [("wo", c - 1), ("sum", c - 1), ("ft", c - 1), ("rt", c - 1)]
                gap = 3 if len(found) > 12 else 0
                for n, it in enumerate(post):
                    found.insert(2 + n * (gap + 1), it) if gap else found.append(it)
            if 0 <= c and c + 2 < NCH:
                found += [(k, c + 2) for k in ("qa", "qb", "kk", "v")]
            return found

        ORDER = []
        for c in range(-1, NCH):
            its = items_of(c)
            if c == -1:
                ORDER += its
                continue
            n_units = 2 * TPC * (c + 1)
            sent = 0
            for n in range(n_units):
                ORDER.append(("unit", c, n // 2, n % 2))
                upto = len(its) * (n + 1) // n_units
                ORDER += its[sent:upto]
                sent = upto
        ORDER += [("wo", NCH - 1), ("sum", NCH - 1), ("ft", NCH - 1), ("rt", NCH - 1)]
        ITEM = {}
        for o in ORDER:
            if o[0] not in ("unit", "sum"):
                ITEM[o] = len(ITEM)

        def adj_count(ic, jg):
            return 16 * (NGRP // RING * ic + jg // RING + 1)

        block = ctx.enter_context(nc.Block())

        @block.sync
        def _(sp):
            for k in range(2):
                h = TILES // 2
                sp.dma_start(xs[:, h * k:h * k + h, :], x[:, h * k:h * k + h, :]).then_inc(s_x[k], 16)
                if k == 0:
                    for dst, src in ((wn[:, :], neigh_w), (w2l[:, :], lin2_t), (wg[:, 1, :], lin1_t),
                                     (ident[:, :], ident_in)):
                        sp.dma_start(dst, src).then_inc(s_w, 16)
            for ic in range(NCH):
                for jg in range(NGRP):
                    if ic or jg >= RING:
                        ip, jp = (ic, jg - RING) if jg >= RING else (ic - 1, jg + NGRP - RING)
                        sp.wait_ge(s_adj_pe, NGRP * ip + jp + 1)
                        if jp < POOL_GRPS:
                            sp.wait_ge(s_adj_pool, POOL_ADDS * ip + max(jp, 1))
                        else:
                            sp.wait_ge(s_adj_dve, ip + 1)
                    sp.dma_start(ring[:, jg % RING, :, :], adj_t[ic, jg, :, :, :]).then_inc(s_adj[jg % RING], 16)
            sp.wait_ge(s_hT, NCH)
            for c in range(NCH + 2):
                if c < NCH:
                    if c >= 2:
                        sp.wait_ge(s_free, ITEM[("kk", c - 2)] + 1)
                    for k, src in enumerate((cos_t, sin_t)):
                        sp.dma_start(cs[:, c % 2, k, :], src[:, CH * c:CH * c + CH]).then_inc(s_cs[c % 2], 16)
                if c == 1:
                    for dst, src in ((w1s[:, :, :], w1_t), (w3s[:, :, :], w3_t),
                                     (tri[:, :, :], tri_in)):
                        sp.dma_start(dst, src).then_inc(s_moe, 16)
                    for k, (o, n) in enumerate(KB):
                        sp.dma_start(w2s[0:n, :, k, :], w2_t[:, o:o + n, :].rearrange("e h c -> h e c")).then_inc(s_moe, 16)
                if 1 <= c <= NCH:
                    d = c - 1
                    b = d % 2
                    raw = hl[:, :, :, :].bitcast(fp32)
                    span = slice(CH * d, CH * d + CH)
                    sp.wait_ge(s_hl, 4 * d + 4)
                    if d >= QS:
                        sp.wait_ge(s_qk, units_before(d - QS + 1))
                    for h in range(NH):
                        for r, part in enumerate((0, 1, 0)):
                            sp.dma_start(qst[HD * r:HD * r + HD, d % QS, h, :].bitcast(fp32),
                                         raw[HD * h:HD * h + HD, 0, part, :]).then_inc(s_stk[b], 16)
                    for h in range(NKV):
                        for r, part in enumerate((0, 0, 1)):
                            sp.dma_start(kst[HD * r:HD * r + HD, h, span].bitcast(fp32),
                                         raw[HD * h:HD * h + HD, 1, part, :]).then_inc(s_stk[b], 16)
            sp.wait_ge(s_out, 16 * NCH)

        @block.gpsimd
        def _(pool):
            nc.gpsimd.memset(kst[MROW:MROW + 1, :, :].bitcast(fp32), 1.0).then_inc(s_fill, 1)
            pool.wait_ge(s_fill, 1)
            nc.gpsimd.memset(v1[:, :, :, HD:2 * HD], 1.0).then_inc(s_fill, 1)
            for ic in range(NCH):
                for k in range(1, POOL_GRPS):
                    if ic == 0 and k == 1:
                        pool.wait_ge(s_fill, 2)
                    if k == 1:
                        pool.wait_ge(s_adj[0], adj_count(ic, 0))
                        if ic:
                            pool.wait_ge(s_fold, 3 * ic - 2)
                    else:
                        pool.wait_ge(s_adj_pool, POOL_ADDS * ic + k - 1)
                    pool.wait_ge(s_adj[k % RING], adj_count(ic, k))
                    a = ring[:, 0, :, :] if k == 1 else acc_p[:, :, :]
                    nc.gpsimd.tensor_tensor(acc_p[:, :, :], a, ring[:, k % RING, :, :],
                                            ALU.add).then_inc(s_adj_pool, 1)

            for c in range(NCH):
                pool.wait_ge(s_free, ITEM[("mt", c)] + 1)
                for h in range(NH):
                    pool.dma_start(qst[MROW:MROW + 1, c % QS, h, :].bitcast(fp32).rearrange("a (t c) -> a t c", c=P),
                                   mrow[TPC * h:TPC * h + TPC, c % 2, :].bitcast(fp32)).then_inc(s_m[c % 2], 16)

        @block.scalar
        def _(act):
            for dst, src in ((masks[:, :, :], mask_in), (ln1s[:, :], ln1), (ln2s[:, :], ln2),
                             (wqs[:, 0, :], wq_t), (wqs[:, 1, :], wqr_t), (wks[:, :], wk_t),
                             (wvs[:, :], wv_t), (wos[:, :], wo_t), (rts[:, :], router_t)):
                act.dma_start(dst, src).then_inc(s_c, 16)
            act.wait_ge(s_one, 3)
            act.wait_ge(s_wgp, 1)
            nc.scalar.copy(wg[:, 0, :], ps[:, 2, 0:P]).then_inc(s_wg, 1)
            for c in range(NCH + 2):
                if c < NCH:
                    b = c % 2
                    act.wait_ge(s_cen, c + 1)
                    nc.scalar.activation(sq[:, b], cen[:, b], ACT.Square).then_inc(s_sq, 1)
                    act.wait_ge(s_var, c + 1)
                    nc.scalar.activation(st[:, b, 3, :], st[:, b, 2, :], ACT.Sqrt, bias=eps5[:, 0:1],
                                         scale=1.0 / C).then_inc(s_std, 1)
                if 1 <= c <= NCH:
                    d = c - 1
                    act.wait_ge(s_xt, d + 1)
                    nc.scalar.copy(xnT[:, d % 2, :], ps[:, 2 + d % 2, :]).then_inc(s_xnT, 1)
                if 2 <= c:
                    d = c - 2
                    act.wait_ge(s_gz, d + 1)
                    bank = 4 + 2 * (d % 2)
                    gz = ps[:, bank:bank + 2, :].rearrange("p b (t s c) -> p (b t) s c", s=2, c=C)
                    nc.scalar.copy(gs[:, TPC * d:TPC * d + TPC, :], gz[:, :, 0, :]).then_inc(s_g, 1)
            act.wait_ge(s_c, 9 * 16)
            for ic in range(NCH):
                act.wait_ge(s_cen, NCH + ic + 1)
                nc.scalar.activation(sq[:, 0], cen[:, 0], ACT.Square).then_inc(s_sq, 1)
                act.wait_ge(s_var, NCH + ic + 1)
                nc.scalar.activation(st[:, 0, 3, :], st[:, 0, 2, :], ACT.Sqrt, bias=eps5[:, 0:1],
                                     scale=1.0 / C).then_inc(s_std, 1)
                act.wait_ge(s_u, 2 * ic + 1)
                nc.scalar.activation(sq[:, 1], us[:, TPC * ic:TPC * ic + TPC, :], ACT.Square).then_inc(s_usq, 1)
                act.wait_ge(s_u, 2 * ic + 2)
                nc.scalar.activation(st[:, 0, 6, :], st[:, 0, 5, :], ACT.Sqrt, bias=eps6[:, 0:1],
                                     scale=1.0 / C).then_inc(s_ustd, 1)
                act.wait_ge(s_ht, ic + 1)
                nc.scalar.activation(hT[:, CH * ic:CH * ic + CH], ps[:, 4, :], ACT.Copy,
                                     scale=ln1s[:, 0:1]).then_inc(s_hT, 1)
            u = 0
            for o in ORDER:
                if o[0] == "unit":
                    _, c, st_, pair = o
                    act.wait_ge(s_qk, u + 1)
                    if u >= PB:
                        act.wait_ge(s_pv, u - PB + 1)
                    lo = max(0, P * (st_ - TPC * c))
                    b = 2 * (u % 2)
                    nc.scalar.activation(pb[:, u % PB, :, lo:CH], ps[:, b:b + 2, lo:CH], ACT.Exp,
                                         scale=SCALE).then_inc(s_exp, 1)
                    u += 1
                elif o[0] == "ft":
                    act.wait_ge(s_ss, o[1] + 1)
                    nc.scalar.activation(sta[:, 1, :], sta[:, 0, :], ACT.Sqrt, bias=eps6[:, 0:1],
                                         scale=1.0 / C).then_inc(s_sd, 1)
            act.wait_ge(s_rm, 1)
            nc.scalar.activation(pr[:, :, :], pr[:, :, :], ACT.Exp).then_inc(s_re, 1)
            for v in range(NCH * NE * len(KB)):
                n = KB[v % len(KB)][1]
                act.wait_ge(s_ab, v + 1)
                if v >= 2:
                    act.wait_ge(s_hh, v - 1)
                nc.scalar.activation(sil[0:n, v % 2, :], ps[0:n, 2 * (v % 2), :], ACT.Silu).then_inc(s_sil, 1)
                if v % (NE * len(KB)) == NE * len(KB) - 1:
                    c = v // (NE * len(KB))
                    if c >= 1:
                        act.wait_ge(s_acc, TPC * NE * c)
                        act.dma_start(out[:, TPC * (c - 1):TPC * c, :], xs[:, TPC * (c - 1):TPC * c, :]).then_inc(s_out, 16)
            act.wait_ge(s_acc, TPC * NE * NCH)
            act.dma_start(out[:, TILES - TPC:TILES, :], xs[:, TILES - TPC:TILES, :]).then_inc(s_out, 16)

        @block.vector
        def _(dve):
            def wide(a):
                return a.unsqueeze(2).broadcast_to([P, TPC, C])

            nc.vector.memset(ones[:, :], 1.0).then_inc(s_one, 1)
            nc.vector.memset(eps5[:, :], 1e-5).then_inc(s_one, 1)
            nc.vector.memset(eps6[:, :], 1e-6).then_inc(s_one, 1)

            small = [0]

            def step(ins):
                small[0] += 1
                ins.then_inc(s_lnst, 1)
                dve.wait_ge(s_lnst, small[0])

            def centre(src, b):
                step(nc.vector.reduce_sum(st[:, b, 0, :], src, X_AXIS))
                step(nc.vector.tensor_scalar_mul(st[:, b, 1, :], st[:, b, 0, :], -1.0 / C))
                nc.vector.tensor_tensor(cen[:, b], src, wide(st[:, b, 1, :]), ALU.add).then_inc(s_cen, 1)

            def variance(n, b):
                dve.wait_ge(s_sq, n)
                nc.vector.reduce_sum(st[:, b, 2, :], sq[:, b], X_AXIS).then_inc(s_var, 1)

            def inverse(n, b):
                dve.wait_ge(s_std, n)
                step(nc.vector.reciprocal(st[:, b, 4, :], st[:, b, 3, :]))

            for c in range(NCH + 2):
                if c < NCH:
                    if c in (0, NCH // 2):
                        dve.wait_ge(s_x[c // (NCH // 2)], 16)
                    centre(xs[:, TPC * c:TPC * c + TPC, :], c % 2)
                if 1 <= c <= NCH:
                    d, b = c - 1, (c - 1) % 2
                    inverse(d + 1, b)
                    if d >= 2:
                        dve.wait_ge(s_xt, d - 1)
                    nc.vector.tensor_tensor(nrm[:, b], cen[:, b], wide(st[:, b, 4, :]), ALU.mult).then_inc(s_xn, 1)
                if c < NCH:
                    variance(c + 1, c % 2)
                if 2 <= c:
                    d = c - 2
                    dve.wait_ge(s_g, d + 1)
                    bank = 4 + 2 * (d % 2)
                    gz = ps[:, bank:bank + 2, :].rearrange("p b (t s c) -> p (b t) s c", s=2, c=C)
                    xc = xs[:, TPC * d:TPC * d + TPC, :]
                    nc.vector.tensor_tensor(xc, xc, gz[:, :, 1, :], ALU.add).then_inc(s_z, 1)

            def fold(ic):
                dve.wait_ge(s_adj[6 % RING], adj_count(ic, 6))
                dve.wait_ge(s_adj[7 % RING], adj_count(ic, 7))
                if ic:
                    dve.wait_ge(s_deg, ic)
                nc.vector.tensor_tensor(acc_v[:, :, :], ring[:, 6 % RING, :, :], ring[:, 7 % RING, :, :],
                                        ALU.add).then_inc(s_adj_dve, 1)
                dve.wait_ge(s_adj_dve, ic + 1)
                dve.wait_ge(s_adj_pool, POOL_ADDS * (ic + 1))
                nc.vector.tensor_tensor(acc_v[:, :, :], acc_v[:, :, :], acc_p[:, :, :], ALU.add).then_inc(s_fold, 1)
                dve.wait_ge(s_fold, 3 * ic + 1)
                nc.vector.tensor_tensor(acc_v[:, 0:2, :], acc_v[:, 0:2, :], acc_v[:, 2:4, :], ALU.add).then_inc(s_fold, 1)
                dve.wait_ge(s_fold, 3 * ic + 2)
                nc.vector.tensor_tensor(acc_v[:, 0, :], acc_v[:, 0, :], acc_v[:, 1, :], ALU.add).then_inc(s_fold, 1)

            def after(ic):
                dve.wait_ge(s_deg, ic + 1)
                nc.vector.tensor_scalar_add(deg[:, :], ps[:, 2, :], 1.0).then_inc(s_rdeg, 1)
                dve.wait_ge(s_rdeg, 2 * ic + 1)
                nc.vector.reciprocal(rdeg[:, :], deg[:, :]).then_inc(s_rdeg, 1)
                dve.wait_ge(s_rdeg, 2 * ic + 2)
                dve.wait_ge(s_adj_pe, NGRP * (ic + 1))
                if ic:
                    dve.wait_ge(s_nat, ic)
                nc.vector.tensor_tensor(aggT[:, :], ps[:, ic % 2, :], rdeg[:, :], ALU.mult).then_inc(s_aggT, 1)
                xc = xs[:, TPC * ic:TPC * ic + TPC, :]
                uc = us[:, TPC * ic:TPC * ic + TPC, :]
                dve.wait_ge(s_nat, ic + 1)
                nc.vector.tensor_tensor(xc, xc, ps[:, 3, :].rearrange("p (t c) -> p t c", c=C),
                                        ALU.add).then_inc(s_x1, 1)
                dve.wait_ge(s_x1, ic + 1)
                centre(xc, 0)
                variance(NCH + ic + 1, 0)
                inverse(NCH + ic + 1, 0)
                nc.vector.tensor_tensor(uc, cen[:, 0], wide(st[:, 0, 4, :]), ALU.mult).then_inc(s_u, 1)
                dve.wait_ge(s_usq, ic + 1)
                nc.vector.reduce_sum(st[:, 0, 5, :], sq[:, 1], X_AXIS).then_inc(s_u, 1)
                dve.wait_ge(s_ustd, ic + 1)
                step(nc.vector.reciprocal(st[:, 0, 7, :], st[:, 0, 6, :]))
                nc.vector.tensor_tensor(nrm[:, 0], uc, wide(st[:, 0, 7, :]), ALU.mult).then_inc(s_hn, 1)

            for ic in range(NCH):
                if ic:
                    after(ic - 1)
                fold(ic)
            after(NCH - 1)

            vec = [0]

            def done(ins):
                vec[0] += 1
                ins.then_inc(s_vec, 1)

            def settle():
                dve.wait_ge(s_vec, vec[0])

            dve.wait_ge(s_c, 9 * 16)
            dve.wait_ge(s_w, 4 * 16)
            nc.vector.tensor_copy(maskb[:, 0:2, :], masks[:, :, :]).then_inc(s_mb, 1)
            nc.vector.tensor_copy(maskb[:, 2, :], ident[:, :]).then_inc(s_mb, 1)
            dve.wait_ge(s_hT, NCH)
            for o in ORDER:
                kind, c = o[0], o[1]
                if kind == "unit":
                    continue
                xc = us[:, TPC * c:TPC * c + TPC, :]
                if kind == "wo":
                    dve.wait_ge(s_pv, units_before(c + 1))
                    if c:
                        dve.wait_ge(s_item, ITEM[("wo", c - 1)] + 1)
                    dve.wait_ge(s_hl, 4 * min(c + 3, NCH))
                    for pair in range(2):
                        nc.vector.reciprocal(rec[:, pair, :], ps[:, 4 + pair, :]).then_inc(s_y, 1)
                    for h in range(NH):
                        dve.wait_ge(s_y, 6 * c + h // 2 + 1)
                        q = 2 * HD * (h % 2)
                        nc.vector.tensor_tensor(yT[HD * h:HD * h + HD, :], ps[q:q + HD, 4 + h // 2, :],
                                                rec[q + HD:q + 2 * HD, h // 2, :], ALU.mult).then_inc(s_y, 1)
                if kind == "sum":
                    settle()
                    nc.vector.reduce_sum(sta[:, 0, :], sqa[:, :, :], X_AXIS).then_inc(s_ss, 1)
                    continue
                if kind == "ft":
                    dve.wait_ge(s_sd, c + 1)
                    done(nc.vector.reciprocal(sta[:, 2, :], sta[:, 1, :]))
                    settle()
                    nc.vector.tensor_tensor(sqa[:, :, :], xc, wide(sta[:, 2, :]), ALU.mult).then_inc(s_fn, 1)
                if kind == "mt":
                    dve.wait_ge(s_free, ITEM[o])
                    nc.vector.reduce_max(mred[:, :], mx[:, :, 0:c + 1], X_AXIS).then_inc(s_mred, 1)
                n = ITEM[o]
                bank = ps[:, 6 + n % 2, :]
                dve.wait_ge(s_item, n + 1)
                if kind == "max":
                    _, _, t, h, k = o
                    w = CH if k < c else P * (t + 1)
                    if c and t == h == k == 0:
                        dve.wait_ge(s_mred, c)
                    nc.vector.reduce_max(mx[:, TPC * h + t, k:k + 1], bank[:, 0:w], X_AXIS).then_inc(s_free, 1)
                elif kind == "mt":
                    if c >= 2:
                        dve.wait_ge(s_m[c % 2], 16 * NH * (c // 2))
                    nc.vector.tensor_scalar_mul(mrow[:, c % 2, :], bank[0:NH * TPC, 0:P], -1.0).then_inc(s_free, 1)
                elif kind == "qa":
                    dve.wait_ge(s_cs[c % 2], 32 * (c // 2 + 1))
                    if c:
                        dve.wait_ge(s_hl, 4 * c)
                    if c >= 3:
                        dve.wait_ge(s_y, 6 * (c - 2))
                    nc.vector.tensor_tensor(ta, bank, cs[:, c % 2, 0, :], ALU.mult).then_inc(s_free, 1)
                elif kind == "qb":
                    nc.vector.tensor_tensor(tb, bank, cs[:, c % 2, 1, :], ALU.mult).then_inc(s_free, 1)
                    dve.wait_ge(s_free, n + 1)
                    done(nc.vector.tensor_tensor(ta, ta, tb, ALU.add))
                    settle()
                    if c:
                        dve.wait_ge(s_stk[(c - 1) % 2], 16 * 18 * ((c + 1) // 2))
                    nc.vector.tensor_copy(hl[:, 0, 0, :], ta).then_inc(s_hl, 1)
                    dve.wait_ge(s_hl, 4 * c + 1)
                    nc.vector.tensor_tensor(hl[:, 0, 1, :], ta, hl[:, 0, 0, :].bitcast(fp32),
                                            ALU.subtract).then_inc(s_hl, 1)
                elif kind == "kk":
                    H = NKV * HD
                    dve.wait_ge(s_hl, 4 * c + 2)
                    done(nc.vector.tensor_tensor(ta[0:H, :], bank[0:H, :], cs[0:H, c % 2, 0, :], ALU.mult))
                    nc.vector.tensor_tensor(tb[0:H, :], bank[H:2 * H, :], cs[H:2 * H, c % 2, 1, :], ALU.mult).then_inc(s_free, 1)
                    settle()
                    dve.wait_ge(s_free, n + 1)
                    done(nc.vector.tensor_tensor(ta[0:H, :], ta[0:H, :], tb[0:H, :], ALU.add))
                    settle()
                    nc.vector.tensor_copy(hl[0:H, 1, 0, :], ta[0:H, :]).then_inc(s_hl, 1)
                    dve.wait_ge(s_hl, 4 * c + 3)
                    nc.vector.tensor_tensor(hl[0:H, 1, 1, :], ta[0:H, :], hl[0:H, 1, 0, :].bitcast(fp32),
                                            ALU.subtract).then_inc(s_hl, 1)
                elif kind == "v":
                    nc.vector.tensor_copy(v1[:, TPC * c:TPC * c + TPC, :, 0:HD],
                                          bank[:, 0:TPC * NKV * HD].rearrange("p (t k d) -> p t k d", t=TPC, k=NKV)).then_inc(s_free, 1)
                elif kind == "wo":
                    nc.vector.tensor_tensor(xc, xc, bank.rearrange("p (t c) -> p t c", c=C), ALU.add).then_inc(s_free, 1)
                    dve.wait_ge(s_free, n + 1)
                    if c:
                        dve.wait_ge(s_item, ITEM[("ft", c - 1)] + 1)
                    done(nc.vector.tensor_tensor(sqa[:, :, :], xc, xc, ALU.mult))
                elif kind == "ft":
                    nc.vector.tensor_scalar(hT[:, CH * c:CH * c + CH], bank, ln2s[:, 0:1], None, ALU.mult).then_inc(s_free, 1)
                elif kind == "rt":
                    nc.vector.tensor_copy(lg[:, TPC * c:TPC * c + TPC, :],
                                          bank[:, 0:TPC * NE].rearrange("p (t e) -> p t e", e=NE)).then_inc(s_free, 1)

            dve.wait_ge(s_free, len(ITEM))

            def over(a, n=NE):
                return a.unsqueeze(2).broadcast_to([P, TILES, n])

            done(nc.vector.reduce_max(rsm[:, 0, :], lg[:, :, :], X_AXIS))
            settle()
            nc.vector.tensor_tensor(pr[:, :, :], lg[:, :, :], over(rsm[:, 0, :]), ALU.subtract).then_inc(s_rm, 1)
            dve.wait_ge(s_re, 1)
            done(nc.vector.reduce_sum(rsm[:, 1, :], pr[:, :, :], X_AXIS))
            settle()
            done(nc.vector.reciprocal(rsm[:, 2, :], rsm[:, 1, :]))
            settle()
            done(nc.vector.tensor_tensor(pr[:, :, :], pr[:, :, :], over(rsm[:, 2, :]), ALU.mult))
            settle()
            other = pr[:, :, :].unsqueeze(2).broadcast_to([P, TILES, NE, NE])
            own = pr[:, :, :].unsqueeze(3).broadcast_to([P, TILES, NE, NE])
            before = tri[:, :, :].unsqueeze(1).broadcast_to([P, TILES, NE, NE])
            dve.wait_ge(s_moe, 16 * 6)
            done(nc.vector.tensor_tensor(cmp, other, own, ALU.is_gt))
            done(nc.vector.tensor_tensor(eqs, other, own, ALU.is_equal))
            settle()
            done(nc.vector.tensor_tensor(eqs, eqs, before, ALU.mult))
            settle()
            done(nc.vector.tensor_tensor(cmp, cmp, eqs, ALU.add))
            settle()
            done(nc.vector.reduce_sum(wt[:, :, :], cmp, X_AXIS))
            settle()
            done(nc.vector.tensor_scalar(wt[:, :, :], wt[:, :, :], 2.0, None, ALU.is_lt))
            settle()
            done(nc.vector.tensor_tensor(wt[:, :, :], wt[:, :, :], pr[:, :, :], ALU.mult))
            settle()
            done(nc.vector.reduce_sum(rsm[:, 3, :], wt[:, :, :], X_AXIS))
            settle()
            done(nc.vector.tensor_scalar_add(rsm[:, 4, :], rsm[:, 3, :], 1e-9))
            settle()
            done(nc.vector.reciprocal(rsm[:, 5, :], rsm[:, 4, :]))
            settle()
            done(nc.vector.tensor_tensor(wt[:, :, :], wt[:, :, :], over(rsm[:, 5, :]), ALU.mult))
            done(nc.vector.tensor_tensor(xs[:, :, :], xs[:, :, :], us[:, :, :], ALU.add))
            settle()

            def down(w):
                c, e = w // NE, w % NE
                dve.wait_ge(s_dn, w + 1)
                for t in range(TPC):
                    if e:
                        dve.wait_ge(s_acc, TPC * (w - 1) + t + 1)
                    row = xs[:, TPC * c + t, :]
                    nc.vector.scalar_tensor_tensor(row, ps[:, 4 + w % 2, P * t:P * t + P],
                                                   wt[:, TPC * c + t, e:e + 1], row,
                                                   ALU.mult, ALU.add).then_inc(s_acc, 1)

            for w in range(NCH * NE):
                for k, (_, n) in enumerate(KB):
                    v = len(KB) * w + k
                    dve.wait_ge(s_sil, v + 1)
                    if w >= 2:
                        dve.wait_ge(s_dn, w - 1)
                    nc.vector.tensor_tensor(hh[0:n, w % 2, k, :], sil[0:n, v % 2, :], ps[0:n, 2 * (v % 2) + 1, :],
                                            ALU.mult).then_inc(s_hh, 1)
                if w:
                    down(w - 1)
            down(NCH * NE - 1)

        @block.tensor
        def _(pe):
            def transposes(bank, src):
                for t in range(TPC):
                    last = nc.tensor.transpose(ps[:, bank, P * t:P * t + P], src(t), ident[:, :])
                return last

            def aggregate(ic, jg):
                pe.wait_ge(s_adj[jg % RING], adj_count(ic, jg))
                if jg == 0 and ic >= 2:
                    pe.wait_ge(s_aggT, ic - 1)
                for q in range(GRP):
                    j = GRP * jg + q
                    last = nc.tensor.matmul(ps[:, ic % 2, :], gs[:, j, :], ring[:, jg % RING, q, :],
                                            start=(j == 0), stop=(j == TILES - 1))
                last.then_inc(s_adj_pe, 1)

            pe.wait_ge(s_w, 64)
            pe.wait_ge(s_one, 1)
            nc.tensor.matmul(ps[:, 2, 0:P], wn[:, :], w2l[:, :], start=True, stop=True).then_inc(s_wgp, 1)
            for c in range(NCH + 2):
                if c < NCH:
                    pe.wait_ge(s_xn, c + 1)
                    if c >= 2:
                        pe.wait_ge(s_xnT, c - 1)
                    if c == 0:
                        pe.wait_ge(s_wg, 1)
                    transposes(2 + c % 2, lambda t: nrm[:, c % 2, t, :]).then_inc(s_xt, 1)
                if 1 <= c <= NCH:
                    d = c - 1
                    pe.wait_ge(s_xnT, d + 1)
                    if d >= 2:
                        pe.wait_ge(s_z, d - 1)
                    for t in range(TPC):
                        bank = 4 + 2 * (d % 2) + t // 2
                        last = nc.tensor.matmul(ps[:, bank, 2 * P * (t % 2):2 * P * (t % 2) + 2 * P],
                                                xnT[:, d % 2, P * t:P * t + P], wg[:, :, :],
                                                start=True, stop=True)
                    last.then_inc(s_gz, 1)
                if 2 <= c:
                    pe.wait_ge(s_g, c - 1)
                    aggregate(0, c - 2)

            def degree(ic):
                pe.wait_ge(s_fold, 3 * ic + 3)
                if ic:
                    pe.wait_ge(s_rdeg, 2 * ic - 1)
                nc.tensor.matmul(ps[:, 2, :], ones[:, :], acc_v[:, 0, :], start=True, stop=True).then_inc(s_deg, 1)

            def natural(ic):
                pe.wait_ge(s_aggT, ic + 1)
                if ic:
                    pe.wait_ge(s_x1, ic)
                transposes(3, lambda t: aggT[:, P * t:P * t + P]).then_inc(s_nat, 1)

            def h_rows(ic):
                pe.wait_ge(s_hn, ic + 1)
                if ic:
                    pe.wait_ge(s_hT, ic)
                transposes(4, lambda t: nrm[:, 0, t, :]).then_inc(s_ht, 1)

            pe.wait_ge(s_z, NCH)
            for ic in range(1, NCH):
                for jg in range(NGRP):
                    aggregate(ic, jg)
                    if jg == 0:
                        pass
                    if jg == 1:
                        degree(ic - 1)
                    if jg == 3:
                        natural(ic - 1)
                    if jg == 6:
                        h_rows(ic - 1)
            degree(NCH - 1)
            natural(NCH - 1)
            h_rows(NCH - 1)

            pe.wait_ge(s_c, 9 * 16)
            pe.wait_ge(s_mb, 2)
            pe.wait_ge(s_fill, 2)
            identb = maskb[:, 2, :]

            def values(u, c, st_, pair):
                pe.wait_ge(s_exp, u + 1)
                if st_ == 0 and c:
                    pe.wait_ge(s_y, 6 * c)
                pe.wait_ge(s_free, ITEM[("v", st_ // TPC)] + 1)
                lo = max(0, P * (st_ - TPC * c))
                for j in range(2):
                    last = nc.tensor.matmul(ps[2 * HD * j:2 * HD * j + 2 * HD, 4 + pair, lo:CH],
                                            v1[:, st_, pair, :], pb[:, u % PB, j, lo:CH],
                                            start=(st_ == 0), stop=(st_ == TPC * (c + 1) - 1))
                last.then_inc(s_pv, 1)

            u = 0
            waiting = None
            for o in ORDER:
                kind, c = o[0], o[1]
                if kind == "unit":
                    _, _, st_, pair = o
                    if st_ == 0 and pair == 0:
                        pe.wait_ge(s_m[c % 2], 16 * NH * (c // 2 + 1))
                    if u >= 2:
                        pe.wait_ge(s_exp, u - 1)
                    lo = max(0, P * (st_ - TPC * c))
                    diagonal = st_ >= TPC * c
                    for j in range(2):
                        h = 2 * pair + j
                        o_ps = ps[:, 2 * (u % 2) + j, :]
                        last = nc.tensor.matmul(o_ps[:, lo:CH], kst[0:MROW + 1, pair, P * st_:P * st_ + P],
                                                qst[0:MROW + 1, c % QS, h, lo:CH],
                                                start=True, stop=not diagonal)
                        if diagonal:
                            last = nc.tensor.matmul(o_ps[:, lo:lo + P], identb, maskb[:, 1, :],
                                                    start=False, stop=True)
                    last.then_inc(s_qk, 1)
                    if waiting:
                        values(*waiting)
                    waiting = (u, c, st_, pair)
                    u += 1
                    continue
                if waiting and (kind, c) == ("wo", NCH - 1):
                    values(*waiting)
                    waiting = None
                if kind == "sum":
                    continue
                n = ITEM[o]
                bank = ps[:, 6 + n % 2, :]
                if n >= 2:
                    pe.wait_ge(s_free, n - 1)
                if kind == "max":
                    _, _, t, h, k = o
                    if t == h == k == 0:
                        pe.wait_ge(s_stk[c % 2], 16 * 18 * (c // 2 + 1))
                    w = CH if k < c else P * (t + 1)
                    last = nc.tensor.matmul(bank[:, 0:w], qst[0:STACK, c % QS, h, P * t:P * t + P],
                                            kst[0:STACK, h // 2, CH * k:CH * k + w],
                                            start=True, stop=(k < c))
                    if k == c:
                        last = nc.tensor.matmul(bank[:, w - P:w], identb, maskb[:, 0, :], start=False, stop=True)
                elif kind == "mt":
                    pe.wait_ge(s_mred, c + 1)
                    last = nc.tensor.matmul(bank[0:NH * TPC, 0:P], mred[:, :], ident[:, :], start=True, stop=True)
                elif kind in ("qa", "qb"):
                    pe.wait_ge(s_hT, NCH)
                    last = nc.tensor.matmul(bank, wqs[:, int(kind == "qb"), :], hT[:, CH * c:CH * c + CH],
                                            start=True, stop=True)
                elif kind == "kk":
                    last = nc.tensor.matmul(bank, wks[:, :], hT[:, CH * c:CH * c + CH], start=True, stop=True)
                elif kind == "v":
                    for t in range(TPC):
                        r = CH * c + P * t
                        last = nc.tensor.matmul(bank[:, NKV * HD * t:NKV * HD * (t + 1)], hT[:, r:r + P], wvs[:, :],
                                                start=True, stop=True)
                elif kind == "wo":
                    pe.wait_ge(s_y, 6 * (c + 1))
                    for t in range(TPC):
                        last = nc.tensor.matmul(bank[:, C * t:C * t + C], yT[:, P * t:P * t + P], wos[:, :],
                                                start=True, stop=True)
                elif kind == "ft":
                    pe.wait_ge(s_fn, c + 1)
                    for t in range(TPC):
                        last = nc.tensor.transpose(bank[:, P * t:P * t + P], sqa[:, t, :], ident[:, :])
                elif kind == "rt":
                    pe.wait_ge(s_free, ITEM[("ft", c)] + 1)
                    for t in range(TPC):
                        r = CH * c + P * t
                        last = nc.tensor.matmul(bank[:, NE * t:NE * t + NE], hT[:, r:r + P], rts[:, :],
                                                start=True, stop=True)
                last.then_inc(s_item, 1)

            pe.wait_ge(s_free, len(ITEM))
            pe.wait_ge(s_moe, 16 * 6)
            pe.wait_ge(s_exp, units_before(NCH))

            def down(w):
                e = w % NE
                pe.wait_ge(s_hh, len(KB) * (w + 1))
                if w >= 2:
                    pe.wait_ge(s_acc, TPC * (w - 1))
                elif w == 0:
                    pe.wait_ge(s_y, 6 * NCH)
                for t in range(TPC):
                    for k, (_, n) in enumerate(KB):
                        last = nc.tensor.matmul(ps[:, 4 + w % 2, P * t:P * t + P], hh[0:n, w % 2, k, P * t:P * t + P],
                                                w2s[0:n, e, k, :], start=(k == 0), stop=(k == len(KB) - 1))
                last.then_inc(s_dn, 1)

            for w in range(NCH * NE):
                c, e = w // NE, w % NE
                for k, (o, n) in enumerate(KB):
                    v = len(KB) * w + k
                    if v >= 2:
                        pe.wait_ge(s_hh, v - 1)
                    for b, ws in enumerate((w1s, w3s)):
                        last = nc.tensor.matmul(ps[0:n, 2 * (v % 2) + b, :], ws[:, e, o:o + n],
                                                hT[:, CH * c:CH * c + CH], start=True, stop=True)
                    last.then_inc(s_ab, 1)
                if w:
                    down(w - 1)
            down(NCH * NE - 1)


def kernel(**inputs):
    import concourse.bacc as bacc
    from concourse.bass_utils import run_bass_kernel_spmd

    a = {k: np.asarray(v) for k, v in inputs.items()}
    lin = a["L0_gnn_lin_W"]
    swapped = (np.arange(HD) + HD // 2) % HD
    wq, wk = a["L0_ffn_wq"], a["L0_ffn_wk"]
    wqr = wq.reshape(NH, HD, C)[:, swapped].reshape(NH * HD, C)
    wkr = wk.reshape(NKV, HD, C)[:, swapped].reshape(NKV * HD, C)
    inv_freq = 1.0 / 10000.0 ** (np.arange(0, HD, 2, dtype=np.float32) / HD)
    freqs = np.outer(np.arange(N, dtype=np.float32), inv_freq)
    emb = np.concatenate([freqs, freqs], axis=-1)
    sign = np.where(np.arange(HD) < HD // 2, -1, 1).astype(np.float32)
    cos = np.tile(np.cos(emb).T, (NH, 1)).astype(np.float32)
    sin = np.tile((np.sin(emb) * sign).T, (NH, 1)).astype(np.float32)
    later = np.where(np.arange(P)[:, None] > np.arange(P)[None, :], np.float32(-1e30), np.float32(0))
    lower = (np.arange(NE)[None, :] < np.arange(NE)[:, None]).astype(np.float32)
    arrays = {
        "x": a["x"].reshape(TILES, P, C).transpose(1, 0, 2),
        "adj_t": a["adj"].reshape(NCH, CH, NGRP, GRP, P).transpose(0, 2, 4, 3, 1),
        "neigh_w": a["L0_gnn_neigh_W"],
        "lin1_t": lin[:, :C].T,
        "lin2_t": lin[:, C:].T,
        "ln1": a["L0_ffn_ln1_w"].reshape(C, 1),
        "ln2": a["L0_ffn_ln2_w"].reshape(C, 1),
        "wq_t": wq.T,
        "wqr_t": wqr.T,
        "wk_t": np.concatenate([wk.T, wkr.T], axis=1),
        "wv_t": a["L0_ffn_wv"].T,
        "wo_t": a["L0_ffn_wo"].T,
        "router_t": a["L0_ffn_router_w"].T,
        "tri_in": np.broadcast_to(lower, (P, NE, NE)),
        "w1_t": a["L0_ffn_w1"].transpose(2, 0, 1),
        "w3_t": a["L0_ffn_w3"].transpose(2, 0, 1),
        "w2_t": a["L0_ffn_w2"].transpose(0, 2, 1),
        "cos_t": cos,
        "sin_t": sin,
        "ident_in": np.eye(P, dtype=np.float32),
        "mask_in": np.stack([later.T, later], axis=1),
    }
    arrays = {k: np.ascontiguousarray(v) for k, v in arrays.items()}
    nc = bacc.Bacc("TRN2", target_bir_lowering=False, num_devices=1)
    args = [nc.dram_tensor(k, v.shape, mybir.dt.from_np(v.dtype), kind="ExternalInput").ap()
            for k, v in arrays.items()]
    out = nc.dram_tensor("out", (P, TILES, C), fp32, kind="ExternalOutput").ap()
    build(nc, *args, out)
    got = run_bass_kernel_spmd(nc, [arrays], core_ids=[0]).results[0]["out"]
    return np.ascontiguousarray(got.transpose(1, 0, 2)).reshape(N, C)
```

```python
import concourse.bass as bass
from concourse import mybir
from concourse.alu_op_type import AluOpType as ALU
from contextlib import ExitStack
import numpy as np

fp32 = mybir.dt.float32
fp32r = mybir.dt.float32r
bf16 = mybir.dt.bfloat16
ACT = mybir.ActivationFunctionType
X_AXIS = mybir.AxisListType.X

P = 128
N = 4096
C = 128
TILES = N // P
CH = 512
NCH = N // CH
TPC = CH // P
NH, NKV, HD = 4, 2, 32
NE, HID = 8, 341
RING = 4
GRP = TPC
NGRP = TILES // GRP
POOL_GRPS = 6
POOL_ADDS = POOL_GRPS - 1
QS = 3
PB = 4
SB = 3
IB = 3
SCALE = 1.0 / float(np.sqrt(np.float32(HD)))
STACK = 3 * HD
MROW = STACK
REG = N + P
ROW = C + 4
NT = 2 * TILES + NE
SPARE = NE * REG
NR = NE + 1
XB = 8
YB = 4
KB = [(0, 128), (128, 128), (256, 85)]


def build(nc, x, adj_t, neigh_w, lin1_t, lin2_t, ln1, ln2, wq_t, wqr_t, wk_t, wv_t, wo_t,
          router_t, tri_in, w13_t, w2_t, cos_t, sin_t, ident_in, mask_in, before_in, base_in, dest_in, tile_in, pad_in, out):
    ctx = ExitStack()
    with ctx:
        def sb(name, shape, dt=fp32):
            return ctx.enter_context(nc.sbuf_tensor(name, shape, dt))

        def sem(name):
            return ctx.enter_context(nc.semaphore(name))

        xs = sb("xs", [P, TILES, C])
        us = sb("us", [P, TILES, C])
        hT = sb("hT", [P, N])
        kst = sb("kst", [P, NKV, N], fp32r)
        v1 = sb("v1", [P, TILES, NKV, 2 * HD])
        ident = sb("ident", [P, P])
        masks = sb("masks", [P, 2, P])
        maskb = sb("maskb", [P, 3, P], bf16)
        ln1s = sb("ln1s", [P, 1])
        ln2s = sb("ln2s", [P, 1])
        eps5 = sb("eps5", [P, 1])
        eps6 = sb("eps6", [P, 1])
        wqs = sb("wqs", [P, 2, P])
        wks = sb("wks", [P, P])
        wvs = sb("wvs", [P, NKV * HD])
        wos = sb("wos", [P, P])
        rts = sb("rts", [P, NE])
        ps = ctx.enter_context(nc.psum_tensor("ps", [P, 8, CH], fp32))

        gn = ExitStack()

        def gsb(name, shape, dt=fp32):
            return gn.enter_context(nc.sbuf_tensor(name, shape, dt))

        ring = gsb("ring", [P, RING, GRP, CH])
        gs = gsb("gs", [P, TILES, C])
        acc_p = gsb("acc_p", [P, GRP, CH])
        acc_v = gsb("acc_v", [P, GRP, CH])
        wn = gsb("wn", [P, P])
        w2l = gsb("w2l", [P, P])
        wg = gsb("wg", [P, 2, P])
        ones = gsb("ones", [P, P])
        cen = gsb("cen", [P, 2, TPC, C])
        nrm = gsb("nrm", [P, 2, TPC, C])
        sq = gsb("sq", [P, 2, TPC, C])
        xnT = gsb("xnT", [P, 2, CH])
        st = gsb("st", [P, 2, 8, TPC])
        deg = gsb("deg", [P, CH])
        rdeg = gsb("rdeg", [P, CH])
        aggT = gsb("aggT", [P, CH])

        s_x = [sem(f"x_loaded{c}") for c in range(2)]
        s_w = sem("gnn_weights_loaded")
        s_c = sem("constants_loaded")
        s_adj = [sem(f"adj_loaded{r}") for r in range(RING)]
        s_adj_pe = sem("adj_multiplied")
        s_adj_pool = sem("adj_summed_pool")
        s_adj_dve = sem("adj_summed_dve")
        s_one = sem("ones_set")
        s_wgp = sem("wg_product")
        s_wg = sem("wg_ready")
        s_cen = sem("x_centred")
        s_sq = sem("squares")
        s_var = sem("variance_sum")
        s_std = sem("deviation")
        s_lnst = sem("ln_steps")
        s_xn = sem("x_normalised")
        s_xt = sem("xn_transposed")
        s_xnT = sem("xnT_ready")
        s_gz = sem("gz_product")
        s_g = sem("g_ready")
        s_z = sem("z_added")
        s_fold = sem("degree_fold")
        s_deg = sem("degree_product")
        s_rdeg = sem("degree_steps")
        s_aggT = sem("aggregate_scaled")
        s_nat = sem("aggregate_transposed")
        s_x1 = sem("x1_steps")
        s_u = sem("u_ready")
        s_usq = sem("u_squares")
        s_ustd = sem("u_deviation")
        s_hn = sem("h_normalised")
        s_ht = sem("h_transposed")
        s_hT = sem("hT_ready")
        s_out = sem("out_stored")
        gn.close()
        qst = sb("qst", [P, QS, NH, CH], fp32r)
        pb = sb("pb", [P, PB, 2, CH])
        cs = sb("cs", [P, 2, 2, CH])
        hl = sb("hl", [P, 2, 2, CH], fp32r)
        mx = sb("mx", [P, NH * TPC, NCH])
        mred = sb("mred", [P, NH * TPC])
        mrow = sb("mrow", [NH * TPC, 2, P], fp32r)
        rec = sb("rec", [P, 2, CH])
        ta, tb = rec[:, 0, :], rec[:, 1, :]
        yT = sb("yT", [P, CH])
        od = sb("od", [P, 2, CH])
        rd = sb("rd", [P, 2, TPC, 2])
        pay = sb("pay", [P, 2, TPC, ROW])
        sqa = sb("sqa", [P, TPC, C])
        yn = sqa[:, :, :].rearrange("p t (h d) -> p t h d", d=HD)
        sta = sb("sta", [P, 4, TPC])
        lg = sb("lg", [P, TPC, NE])
        small4 = sb("small4", [P, 4, TPC])
        cmp = sb("cmp", [P, 2, TPC, NE, NE])
        rank = sb("rank", [P, TPC, NE])
        first = sb("first", [P, 2, TPC, NE])
        share = sb("share", [P, 2, TPC, NE])
        two = sb("two", [P, 2, TPC])
        chosen = sb("chosen", [P, TPC, NE], bf16)
        place = sb("place", [P, TPC, NE])
        run = sb("run", [P, NE])
        slot = sb("slot", [P, 2, TPC], mybir.dt.int32)
        tri = sb("tri", [P, NE, NE])
        beforef = sb("beforef", [P, 2, P])
        beforeb = sb("beforeb", [P, 2, P], bf16)
        base = sb("base", [P, NE])
        dest = sb("dest", [P, 2, TILES], mybir.dt.int32)
        tiles = sb("tiles", [1, N // P + NT + 2 * NR])
        tb1 = cs[0:1, :, :, :].rearrange("p a b c -> p (a b c)")[:, 0:3 * NT * NR].rearrange(
            "p (a n e) -> p a n e", a=3, e=NR)
        tb2 = sb("tb2", [1, 6, NR])
        tb3 = sb("tb3", [1, 2, NT])
        table = sb("table", [1, 2, NT], mybir.dt.int32)
        ends = sb("ends", [1, NE], mybir.dt.int32)
        w13 = sb("w13", [P, NE, 2 * HID])
        w2s = hT[:, 0:NE * len(KB) * C].rearrange("p (e k c) -> p e k c", e=NE, c=C)
        flat = pb[:, :, :, :].rearrange("p a b c -> p (a b c)")
        used = [0]

        def carve(*shape):
            n = int(np.prod(shape))
            view = flat[:, used[0]:used[0] + n]
            used[0] += n
            names = "abc"[:len(shape)]
            return view.rearrange("p (" + " ".join(names) + ") -> p " + " ".join(names),
                                  **dict(zip(names[1:], shape[1:])))

        xt = carve(XB, ROW)
        xtT = carve(2, P)
        sil = carve(2, HID)
        hh = carve(2, HID)
        hhT = carve(2, len(KB), P)
        yo = carve(YB, C)
        fin = v1[:, 0:TILES // 2, :, :].rearrange("p t k d -> p (t k d)").rearrange(
            "p (b t r c) -> p b t r c", b=2, t=TPC, r=2)

        x_rows = nc.dram_tensor("dispatched_rows", [SPARE + NE * P, ROW], fp32, kind="Internal").ap()
        y_rows = nc.dram_tensor("result_rows", [2 * N + 2 * NE * P, C], fp32, kind="Internal").ap()

        s_cs = [sem(f"tables_loaded{b}") for b in range(2)]
        s_stk = [sem(f"stacks_filled{b}") for b in range(2)]
        s_m = [sem(f"maxima_placed{b}") for b in range(2)]
        s_moe = sem("expert_weights_loaded")
        s_mb = sem("masks_ready")
        s_fill = sem("ones_filled")
        s_item = sem("item_ready")
        s_free = sem("item_read")
        s_vec = sem("vector_steps")
        s_hl = sem("split_ready")
        s_mred = sem("maxima_reduced")
        s_qk = sem("scores_ready")
        s_exp = sem("probs_ready")
        s_pv = sem("values_added")
        s_y = sem("y_steps")
        s_ss = sem("attention_squares")
        s_sd = sem("attention_deviation")
        s_fn = sem("flat_normalised")
        s_rm = sem("router_shifted")
        s_re = sem("router_exp")
        s_rc = sem("router_constants_loaded")
        s_bb = sem("router_constants_ready")
        s_cp = sem("second_copy")
        s_sel = sem("experts_chosen")
        s_slot = sem("slots_ready")
        s_disp = sem("rows_dispatched")
        s_tab = sem("table_ready")
        s_pad = sem("padding_stored")
        s_ld = [sem(f"tile_loaded{k}") for k in range(XB)]
        s_ut = sem("tile_transposed")
        s_us = sem("tile_scaled")
        s_up = sem("up_products")
        s_sil = sem("silu_ready")
        s_hh = sem("hidden_ready")
        s_hp = sem("hidden_transposed")
        s_hs = sem("hiddenT_ready")
        s_dn = sem("down_products")
        s_yo = sem("result_ready")
        s_res = [sem(f"result_stored{k}") for k in range(YB)]
        s_fin = [sem(f"results_loaded{k}") for k in range(2)]
        s_sum = sem("results_added")
        s_base = sem("residuals_added")

        def units_before(c):
            return sum(2 * TPC * (k + 1) for k in range(c))

        AFTER = ("to0", "to1", "ty", "wo", "sum", "ft", "rt", "rx", "cu")

        def items_of(c):
            scores = [("max", c + 1, t, h, k) for t in range(TPC) for h in range(NH) for k in range(c + 2)]
            project = ("qa", "qb", "kk", "v")
            if c == -1:
                return [(k, 0) for k in project] + [(k, 1) for k in project] + scores + [("mt", 0)]
            thin = [(k, c - 1) for k in AFTER] if c else []
            if c + 2 < NCH:
                thin[5:5] = [(k, c + 2) for k in project]
            if c + 1 >= NCH:
                return thin
            room = len(scores) - 8 - 20
            gap = min(3, max(1, room // max(1, len(thin))))
            for n, it in enumerate(thin):
                found_at = 8 + (gap + 1) * n + (20 if it[0] == "cu" else 0)
                scores.insert(min(found_at, len(scores)), it)
            return scores + [("mt", c + 1)]

        ORDER = []
        for c in range(-1, NCH):
            its = items_of(c)
            if c == -1:
                ORDER += its
                continue
            n_units = 2 * TPC * (c + 1)
            sent = 0
            for n in range(2 * n_units):
                if n % 2 == 0:
                    ORDER.append(("unit", c, n // 4, n // 2 % 2))
                elif c or n > 1:
                    ORDER.append(("values",) + last_unit)
                if n % 2 == 1:
                    last_unit = (c, n // 4, n // 2 % 2)
                upto = min(len(its), len(its) * (n + 1) * 8 // (2 * n_units * 7))
                ORDER += its[sent:upto]
                sent = upto
        ORDER.append(("values",) + last_unit)
        ORDER += [(k, NCH - 1) for k in AFTER]
        ITEM = {}
        for o in ORDER:
            if o[0] not in ("unit", "values", "sum", "rx"):
                ITEM[o] = len(ITEM)

        def adj_count(ic, jg):
            return 16 * (NGRP // RING * ic + jg // RING + 1)

        block = ctx.enter_context(nc.Block())

        @block.sync
        def _(sp):
            for k in range(2):
                h = TILES // 2
                sp.dma_start(xs[:, h * k:h * k + h, :], x[:, h * k:h * k + h, :]).then_inc(s_x[k], 16)
                if k == 0:
                    for dst, src in ((wn[:, :], neigh_w), (w2l[:, :], lin2_t), (wg[:, 1, :], lin1_t),
                                     (ident[:, :], ident_in)):
                        sp.dma_start(dst, src).then_inc(s_w, 16)
            for ic in range(NCH):
                for jg in range(NGRP):
                    if ic or jg >= RING:
                        ip, jp = (ic, jg - RING) if jg >= RING else (ic - 1, jg + NGRP - RING)
                        sp.wait_ge(s_adj_pe, NGRP * ip + jp + 1)
                        if jp < POOL_GRPS:
                            sp.wait_ge(s_adj_pool, POOL_ADDS * ip + max(jp, 1))
                        else:
                            sp.wait_ge(s_adj_dve, ip + 1)
                    sp.dma_start(ring[:, jg % RING, :, :], adj_t[ic, jg, :, :, :]).then_inc(s_adj[jg % RING], 16)
            sp.wait_ge(s_hT, NCH)
            def tables(c):
                if c >= 2:
                    sp.wait_ge(s_free, ITEM[("kk", c - 2)] + 1)
                for k, src in enumerate((cos_t, sin_t)):
                    sp.dma_start(cs[:, c % 2, k, :], src[:, CH * c:CH * c + CH]).then_inc(s_cs[c % 2], 16)

            def stacks(c):
                b = c % 2
                raw = hl[:, :, :, :].bitcast(fp32)
                span = slice(CH * c, CH * c + CH)
                sp.wait_ge(s_hl, 4 * c + 4)
                if c >= QS:
                    sp.wait_ge(s_qk, 2 * units_before(c - QS + 1))
                for h in range(NH):
                    for r, part in enumerate((0, 1, 0)):
                        sp.dma_start(qst[HD * r:HD * r + HD, c % QS, h, :].bitcast(fp32),
                                     raw[HD * h:HD * h + HD, 0, part, :]).then_inc(s_stk[b], 16)
                for h in range(NKV):
                    for r, part in enumerate((0, 0, 1)):
                        sp.dma_start(kst[HD * r:HD * r + HD, h, span].bitcast(fp32),
                                     raw[HD * h:HD * h + HD, 1, part, :]).then_inc(s_stk[b], 16)

            def maxima(c):
                sp.wait_ge(s_free, ITEM[("mt", c)] + 1)
                for h in range(NH):
                    sp.dma_start(qst[MROW:MROW + 1, c % QS, h, :].bitcast(fp32).rearrange("a (t c) -> a t c", c=P),
                                 mrow[TPC * h:TPC * h + TPC, c % 2, :].bitcast(fp32)).then_inc(s_m[c % 2], 16)

            tables(0)
            tables(1)
            for dst, src in ((tri[:, :, :], tri_in), (beforef[:, :, :], before_in), (base[:, :], base_in),
                             (dest[:, :, :], dest_in), (tiles[:, :], tile_in)):
                sp.dma_start(dst, src).then_inc(s_rc, 16)
            stacks(0)
            stacks(1)
            sp.dma_start(w13[:, :, :], w13_t).then_inc(s_moe, 16)
            maxima(0)
            for c in range(NCH - 1):
                if c + 2 < NCH:
                    tables(c + 2)
                    stacks(c + 2)
                maxima(c + 1)
                if c + 2 == NCH - 1:
                    sp.wait_ge(s_item, ITEM[("v", NCH - 1)] + 1)
                    for k, (o, n) in enumerate(KB):
                        sp.dma_start(w2s[0:n, :, k, :], w2_t[:, o:o + n, :].rearrange("e h c -> h e c")).then_inc(s_moe, 16)

            sp.wait_ge(s_disp, 16 * 2 * TILES)
            sp.wait_ge(s_tab, 2)
            end_rows = [sp.alloc_register(f"end_row{e}") for e in range(NE)]
            sp.load(end_rows, ends[0:1, :])
            for e in range(NE):
                end = sp.snap(end_rows[e], min_val=e * REG, max_val=e * REG + N)
                sp.dma_start(x_rows[bass.ds(end, P), :], pad_in[e, :, :]).then_inc(s_pad, 16)
            sp.dma_start(x_rows[SPARE:SPARE + NE * P, :], pad_in[NE:2 * NE, :, :].rearrange("e p r -> (e p) r")).then_inc(s_pad, 16)
            sp.wait_ge(s_pad, 16 * (NE + 1))

            first_rows = [sp.alloc_register(f"first_row{k}") for k in range(XB)]

            def rows_of(i):
                sp.load(first_rows, table[0:1, 1, bass.ds(XB * i, XB)])

            def load(i, k):
                if not isinstance(i, int) or i:
                    sp.wait_ge(s_res[k % YB], 16 * (XB // YB * (i - 1) + k // YB + 1))
                row = sp.snap(first_rows[k], min_val=0, max_val=SPARE + (NE - 1) * P)
                sp.dma_start(xt[:, k, :], x_rows[bass.ds(row, P), :]).then_inc(s_ld[k], 16)

            rows_of(0)
            for k in range(XB):
                load(0, k)
            with sp.Fori(1, NT // XB) as i:
                rows_of(i)
                for k in range(XB):
                    load(i, k)
            for k in range(YB):
                sp.wait_ge(s_res[k], 16 * NT // YB)
            for c in range(NCH):
                if c >= 2:
                    sp.wait_ge(s_sum, 2 * (c - 1))
                sp.dma_start(fin[:, c % 2], y_rows[2 * CH * c:2 * CH * c + 2 * CH, :].rearrange(
                    "(t p r) c -> p t r c", p=P, r=2)).then_inc(s_fin[c % 2], 16)
            sp.wait_ge(s_out, 16 * NCH)

        @block.gpsimd
        def _(pool):
            nc.gpsimd.memset(kst[MROW:MROW + 1, :, :].bitcast(fp32), 1.0).then_inc(s_fill, 1)
            pool.wait_ge(s_fill, 1)
            nc.gpsimd.memset(v1[:, :, :, HD:2 * HD], 1.0).then_inc(s_fill, 1)
            for ic in range(NCH):
                for k in range(1, POOL_GRPS):
                    if ic == 0 and k == 1:
                        pool.wait_ge(s_fill, 2)
                    if k == 1:
                        pool.wait_ge(s_adj[0], adj_count(ic, 0))
                        if ic:
                            pool.wait_ge(s_fold, 3 * ic - 2)
                    else:
                        pool.wait_ge(s_adj_pool, POOL_ADDS * ic + k - 1)
                    pool.wait_ge(s_adj[k % RING], adj_count(ic, k))
                    a = ring[:, 0, :, :] if k == 1 else acc_p[:, :, :]
                    nc.gpsimd.tensor_tensor(acc_p[:, :, :], a, ring[:, k % RING, :, :],
                                            ALU.add).then_inc(s_adj_pool, 1)

            for c in range(NCH):
                pool.wait_ge(s_slot, c + 1)
                pool.wait_ge(s_cp, c + 1)
                for t in range(TPC):
                    for r in range(2):
                        pool.indirect_dma_start(
                            out=x_rows[:, :],
                            out_offset=bass.IndirectOffsetOnAxis(ap=slot[:, r, t:t + 1].bitcast(mybir.dt.uint32), axis=0),
                            in_=pay[:, r, t, :], in_offset=None).then_inc(s_disp, 16)

            def store(i, k):
                pool.wait_ge(s_yo, XB * i + k + 1)
                pool.indirect_dma_start(
                    out=y_rows[:, :],
                    out_offset=bass.IndirectOffsetOnAxis(ap=xt[:, k, C + 1:C + 2].bitcast(mybir.dt.uint32), axis=0),
                    in_=yo[:, k % YB, :], in_offset=None).then_inc(s_res[k % YB], 16)

            for i in range(NT // XB):
                for k in range(XB):
                    store(i, k)

        @block.scalar
        def _(act):
            for dst, src in ((masks[:, :, :], mask_in), (ln1s[:, :], ln1), (ln2s[:, :], ln2),
                             (wqs[:, 0, :], wq_t), (wqs[:, 1, :], wqr_t), (wks[:, :], wk_t),
                             (wvs[:, :], wv_t), (wos[:, :], wo_t), (rts[:, :], router_t)):
                act.dma_start(dst, src).then_inc(s_c, 16)
            act.wait_ge(s_one, 3)
            act.wait_ge(s_wgp, 1)
            nc.scalar.copy(wg[:, 0, :], ps[:, 2, 0:P]).then_inc(s_wg, 1)
            for c in range(NCH + 2):
                if c < NCH:
                    b = c % 2
                    act.wait_ge(s_cen, c + 1)
                    nc.scalar.activation(sq[:, b], cen[:, b], ACT.Square).then_inc(s_sq, 1)
                    act.wait_ge(s_var, c + 1)
                    nc.scalar.activation(st[:, b, 3, :], st[:, b, 2, :], ACT.Sqrt, bias=eps5[:, 0:1],
                                         scale=1.0 / C).then_inc(s_std, 1)
                if 1 <= c <= NCH:
                    d = c - 1
                    act.wait_ge(s_xt, d + 1)
                    nc.scalar.copy(xnT[:, d % 2, :], ps[:, 2 + d % 2, :]).then_inc(s_xnT, 1)
                if 2 <= c:
                    d = c - 2
                    act.wait_ge(s_gz, d + 1)
                    bank = 4 + 2 * (d % 2)
                    gz = ps[:, bank:bank + 2, :].rearrange("p b (t s c) -> p (b t) s c", s=2, c=C)
                    nc.scalar.copy(gs[:, TPC * d:TPC * d + TPC, :], gz[:, :, 0, :]).then_inc(s_g, 1)
            act.wait_ge(s_c, 9 * 16)
            for ic in range(NCH):
                act.wait_ge(s_cen, NCH + ic + 1)
                nc.scalar.activation(sq[:, 0], cen[:, 0], ACT.Square).then_inc(s_sq, 1)
                act.wait_ge(s_var, NCH + ic + 1)
                nc.scalar.activation(st[:, 0, 3, :], st[:, 0, 2, :], ACT.Sqrt, bias=eps5[:, 0:1],
                                     scale=1.0 / C).then_inc(s_std, 1)
                act.wait_ge(s_u, 2 * ic + 1)
                nc.scalar.activation(sq[:, 1], us[:, TPC * ic:TPC * ic + TPC, :], ACT.Square).then_inc(s_usq, 1)
                act.wait_ge(s_u, 2 * ic + 2)
                nc.scalar.activation(st[:, 0, 6, :], st[:, 0, 5, :], ACT.Sqrt, bias=eps6[:, 0:1],
                                     scale=1.0 / C).then_inc(s_ustd, 1)
                act.wait_ge(s_ht, ic + 1)
                nc.scalar.activation(hT[:, CH * ic:CH * ic + CH], ps[:, 4, :], ACT.Copy,
                                     scale=ln1s[:, 0:1]).then_inc(s_hT, 1)
            def evacuate(c):
                act.wait_ge(s_pv, units_before(c + 1))
                if c:
                    act.wait_ge(s_item, ITEM[("to1", c - 1)] + 1)
                nc.scalar.copy(od[:, :, :], ps[:, SB:SB + 2, :]).then_inc(s_y, 1)

            u = 0
            for o in ORDER:
                if o[0] == "unit":
                    _, c, st_, pair = o
                    if u >= PB:
                        act.wait_ge(s_pv, u - PB + 1)
                    lo = max(0, P * (st_ - TPC * c))
                    for j in range(2):
                        act.wait_ge(s_qk, 2 * u + j + 1)
                        nc.scalar.activation(pb[:, u % PB, j, lo:CH], ps[:, (2 * u + j) % SB, lo:CH], ACT.Exp,
                                             scale=SCALE).then_inc(s_exp, 1)
                    u += 1
                    if c and (st_, pair) == (0, 0):
                        evacuate(c - 1)
                elif o[0] == "to0" and o[1] == NCH - 1:
                    evacuate(NCH - 1)
                elif o[0] == "ft":
                    act.wait_ge(s_ss, o[1] + 1)
                    nc.scalar.activation(sta[:, 1, :], sta[:, 0, :], ACT.Sqrt, bias=eps6[:, 0:1],
                                         scale=1.0 / C).then_inc(s_sd, 1)
                elif o[0] == "rx":
                    c = o[1]
                    act.wait_ge(s_rm, c + 1)
                    nc.scalar.activation(lg[:, :, :], lg[:, :, :], ACT.Exp).then_inc(s_re, 1)
                    if c:
                        act.wait_ge(s_disp, 16 * 2 * TPC * c)
                    nc.scalar.copy(pay[:, 1, :, 0:C], pay[:, 0, :, 0:C]).then_inc(s_cp, 1)
            def step(i, k, scale=True, gate=True):
                s = XB * i + k
                if scale:
                    act.wait_ge(s_ut, s + 2)
                    if k >= 1 or not isinstance(i, int) or i:
                        act.wait_ge(s_up, s)
                    nc.scalar.activation(xtT[:, (k + 1) % 2, :], ps[:, (k + 1) % 2, 0:P], ACT.Copy,
                                         scale=ln2s[:, 0:1]).then_inc(s_us, 1)
                if gate:
                    act.wait_ge(s_up, s + 1)
                    if k >= 2 or not isinstance(i, int) or i:
                        act.wait_ge(s_hh, s - 1)
                    nc.scalar.activation(sil[:, k % 2, :], ps[:, 2 + 2 * (k % 2), 0:HID], ACT.Silu).then_inc(s_sil, 1)

            act.wait_ge(s_ut, 1)
            nc.scalar.activation(xtT[:, 0, :], ps[:, 0, 0:P], ACT.Copy, scale=ln2s[:, 0:1]).then_inc(s_us, 1)
            for k in range(XB):
                step(0, k)
            with act.Fori(1, NT // XB - 1) as i:
                for k in range(XB):
                    step(i, k)
            for k in range(XB):
                step(NT // XB - 1, k, scale=k + 1 < XB)
            for c in range(NCH):
                act.wait_ge(s_sum, 2 * c + 2)
                act.dma_start(out[:, TPC * c:TPC * c + TPC, :], xs[:, TPC * c:TPC * c + TPC, :]).then_inc(s_out, 16)

        @block.vector
        def _(dve):
            def wide(a):
                return a.unsqueeze(2).broadcast_to([P, TPC, C])

            nc.vector.memset(ones[:, :], 1.0).then_inc(s_one, 1)
            nc.vector.memset(eps5[:, :], 1e-5).then_inc(s_one, 1)
            nc.vector.memset(eps6[:, :], 1e-6).then_inc(s_one, 1)

            small = [0]

            def step(ins):
                small[0] += 1
                ins.then_inc(s_lnst, 1)
                dve.wait_ge(s_lnst, small[0])

            def centre(src, b):
                step(nc.vector.reduce_sum(st[:, b, 0, :], src, X_AXIS))
                step(nc.vector.tensor_scalar_mul(st[:, b, 1, :], st[:, b, 0, :], -1.0 / C))
                nc.vector.tensor_tensor(cen[:, b], src, wide(st[:, b, 1, :]), ALU.add).then_inc(s_cen, 1)

            def variance(n, b):
                dve.wait_ge(s_sq, n)
                nc.vector.reduce_sum(st[:, b, 2, :], sq[:, b], X_AXIS).then_inc(s_var, 1)

            def inverse(n, b):
                dve.wait_ge(s_std, n)
                step(nc.vector.reciprocal(st[:, b, 4, :], st[:, b, 3, :]))

            for c in range(NCH + 2):
                if c < NCH:
                    if c in (0, NCH // 2):
                        dve.wait_ge(s_x[c // (NCH // 2)], 16)
                    centre(xs[:, TPC * c:TPC * c + TPC, :], c % 2)
                if 1 <= c <= NCH:
                    d, b = c - 1, (c - 1) % 2
                    inverse(d + 1, b)
                    if d >= 2:
                        dve.wait_ge(s_xt, d - 1)
                    nc.vector.tensor_tensor(nrm[:, b], cen[:, b], wide(st[:, b, 4, :]), ALU.mult).then_inc(s_xn, 1)
                if c < NCH:
                    variance(c + 1, c % 2)
                if 2 <= c:
                    d = c - 2
                    dve.wait_ge(s_g, d + 1)
                    bank = 4 + 2 * (d % 2)
                    gz = ps[:, bank:bank + 2, :].rearrange("p b (t s c) -> p (b t) s c", s=2, c=C)
                    xc = xs[:, TPC * d:TPC * d + TPC, :]
                    nc.vector.tensor_tensor(xc, xc, gz[:, :, 1, :], ALU.add).then_inc(s_z, 1)

            def fold(ic):
                dve.wait_ge(s_adj[6 % RING], adj_count(ic, 6))
                dve.wait_ge(s_adj[7 % RING], adj_count(ic, 7))
                if ic:
                    dve.wait_ge(s_deg, ic)
                nc.vector.tensor_tensor(acc_v[:, :, :], ring[:, 6 % RING, :, :], ring[:, 7 % RING, :, :],
                                        ALU.add).then_inc(s_adj_dve, 1)
                dve.wait_ge(s_adj_dve, ic + 1)
                dve.wait_ge(s_adj_pool, POOL_ADDS * (ic + 1))
                nc.vector.tensor_tensor(acc_v[:, :, :], acc_v[:, :, :], acc_p[:, :, :], ALU.add).then_inc(s_fold, 1)
                dve.wait_ge(s_fold, 3 * ic + 1)
                nc.vector.tensor_tensor(acc_v[:, 0:2, :], acc_v[:, 0:2, :], acc_v[:, 2:4, :], ALU.add).then_inc(s_fold, 1)
                dve.wait_ge(s_fold, 3 * ic + 2)
                nc.vector.tensor_tensor(acc_v[:, 0, :], acc_v[:, 0, :], acc_v[:, 1, :], ALU.add).then_inc(s_fold, 1)

            def after(ic):
                dve.wait_ge(s_deg, ic + 1)
                nc.vector.tensor_scalar_add(deg[:, :], ps[:, 2, :], 1.0).then_inc(s_rdeg, 1)
                dve.wait_ge(s_rdeg, 2 * ic + 1)
                nc.vector.reciprocal(rdeg[:, :], deg[:, :]).then_inc(s_rdeg, 1)
                dve.wait_ge(s_rdeg, 2 * ic + 2)
                dve.wait_ge(s_adj_pe, NGRP * (ic + 1))
                if ic:
                    dve.wait_ge(s_nat, ic)
                nc.vector.tensor_tensor(aggT[:, :], ps[:, ic % 2, :], rdeg[:, :], ALU.mult).then_inc(s_aggT, 1)
                xc = xs[:, TPC * ic:TPC * ic + TPC, :]
                uc = us[:, TPC * ic:TPC * ic + TPC, :]
                dve.wait_ge(s_nat, ic + 1)
                nc.vector.tensor_tensor(xc, xc, ps[:, 3, :].rearrange("p (t c) -> p t c", c=C),
                                        ALU.add).then_inc(s_x1, 1)
                dve.wait_ge(s_x1, ic + 1)
                centre(xc, 0)
                variance(NCH + ic + 1, 0)
                inverse(NCH + ic + 1, 0)
                nc.vector.tensor_tensor(uc, cen[:, 0], wide(st[:, 0, 4, :]), ALU.mult).then_inc(s_u, 1)
                dve.wait_ge(s_usq, ic + 1)
                nc.vector.reduce_sum(st[:, 0, 5, :], sq[:, 1], X_AXIS).then_inc(s_u, 1)
                dve.wait_ge(s_ustd, ic + 1)
                step(nc.vector.reciprocal(st[:, 0, 7, :], st[:, 0, 6, :]))
                nc.vector.tensor_tensor(nrm[:, 0], uc, wide(st[:, 0, 7, :]), ALU.mult).then_inc(s_hn, 1)

            for ic in range(NCH):
                if ic:
                    after(ic - 1)
                fold(ic)
            after(NCH - 1)

            vec = [0]

            def done(ins):
                vec[0] += 1
                ins.then_inc(s_vec, 1)

            def settle():
                dve.wait_ge(s_vec, vec[0])

            routing = iter(())

            def over(a, n=NE):
                return a.unsqueeze(2).broadcast_to([P, TPC, n])

            def route(c):
                dve.wait_ge(s_re, c + 1)
                done(nc.vector.reduce_sum(small4[:, 1, :], lg[:, :, :], X_AXIS))
                yield
                settle()
                done(nc.vector.reciprocal(small4[:, 2, :], small4[:, 1, :]))
                yield
                settle()
                done(nc.vector.tensor_tensor(lg[:, :, :], lg[:, :, :], over(small4[:, 2, :]), ALU.mult))
                yield
                settle()
                other = lg[:, :, :].unsqueeze(2).broadcast_to([P, TPC, NE, NE])
                own = lg[:, :, :].unsqueeze(3).broadcast_to([P, TPC, NE, NE])
                lower = tri[:, :, :].unsqueeze(1).broadcast_to([P, TPC, NE, NE])
                done(nc.vector.tensor_tensor(cmp[:, 0], other, own, ALU.is_gt))
                done(nc.vector.tensor_tensor(cmp[:, 1], other, own, ALU.is_equal))
                yield
                settle()
                done(nc.vector.tensor_tensor(cmp[:, 1], cmp[:, 1], lower, ALU.mult))
                yield
                settle()
                done(nc.vector.tensor_tensor(cmp[:, 0], cmp[:, 0], cmp[:, 1], ALU.add))
                yield
                settle()
                done(nc.vector.reduce_sum(rank[:, :, :], cmp[:, 0], X_AXIS))
                yield
                settle()
                nc.vector.tensor_scalar(chosen[:, :, :], rank[:, :, :], 2.0, None, ALU.is_lt).then_inc(s_sel, 1)
                for r in range(2):
                    done(nc.vector.tensor_scalar(first[:, r], rank[:, :, :], float(r), None, ALU.is_equal))
                yield
                settle()
                done(nc.vector.tensor_tensor(share[:, :, :, :], first[:, :, :, :],
                                             lg[:, :, :].unsqueeze(1).broadcast_to([P, 2, TPC, NE]), ALU.mult))
                yield
                settle()
                done(nc.vector.reduce_sum(two[:, :, :], share[:, :, :, :], X_AXIS))
                yield
                settle()
                done(nc.vector.tensor_tensor(small4[:, 3, :], two[:, 0, :], two[:, 1, :], ALU.add))
                yield
                settle()
                done(nc.vector.tensor_scalar_add(small4[:, 3, :], small4[:, 3, :], 1e-9))
                yield
                settle()
                done(nc.vector.reciprocal(small4[:, 1, :], small4[:, 3, :]))
                yield
                settle()
                if c:
                    dve.wait_ge(s_disp, 16 * 2 * TPC * c)
                done(nc.vector.tensor_tensor(pay[:, :, :, C], two[:, :, :],
                                             small4[:, 1, :].unsqueeze(1).broadcast_to([P, 2, TPC]), ALU.mult))
                done(nc.vector.tensor_copy(pay[:, :, :, C + 1].bitcast(mybir.dt.int32),
                                           dest[:, :, TPC * c:TPC * c + TPC]))

            dve.wait_ge(s_c, 9 * 16)
            dve.wait_ge(s_w, 4 * 16)
            dve.wait_ge(s_rc, 5 * 16)
            done(nc.vector.tensor_copy(beforeb[:, :, :], beforef[:, :, :]))
            done(nc.vector.tensor_copy(run[:, :], base[:, :]))
            nc.vector.memset(pay[:, :, :, C:ROW], 0.0).then_inc(s_bb, 1)
            nc.vector.tensor_copy(maskb[:, 0:2, :], masks[:, :, :]).then_inc(s_mb, 1)
            nc.vector.tensor_copy(maskb[:, 2, :], ident[:, :]).then_inc(s_mb, 1)
            dve.wait_ge(s_hT, NCH)
            for o in ORDER:
                kind, c = o[0], o[1]
                if kind in ("unit", "values"):
                    continue
                xc = us[:, TPC * c:TPC * c + TPC, :]
                if kind == "sum":
                    settle()
                    nc.vector.reduce_sum(sta[:, 0, :], sqa[:, :, :], X_AXIS).then_inc(s_ss, 1)
                    continue
                if kind == "rx":
                    routing = route(c)
                    continue
                if kind == "cu":
                    for _ in routing:
                        pass
                if kind == "ft":
                    dve.wait_ge(s_sd, c + 1)
                    done(nc.vector.reciprocal(sta[:, 2, :], sta[:, 1, :]))
                    settle()
                    if c:
                        dve.wait_ge(s_disp, 16 * 2 * TPC * c)
                    nc.vector.tensor_tensor(pay[:, 0, :, 0:C], xc, wide(sta[:, 2, :]), ALU.mult).then_inc(s_fn, 1)
                if kind == "mt":
                    dve.wait_ge(s_free, ITEM[o])
                    nc.vector.reduce_max(mred[:, :], mx[:, :, 0:c + 1], X_AXIS).then_inc(s_mred, 1)
                n = ITEM[o]
                bank = ps[:, SB + 2 + n % IB, :]
                dve.wait_ge(s_item, n + 1)
                if kind == "max":
                    _, _, t, h, k = o
                    w = CH if k < c else P * (t + 1)
                    if c and t == h == k == 0:
                        dve.wait_ge(s_mred, c)
                    nc.vector.reduce_max(mx[:, TPC * h + t, k:k + 1], bank[:, 0:w], X_AXIS).then_inc(s_free, 1)
                    next(routing, None)
                elif kind == "mt":
                    if c >= 2:
                        dve.wait_ge(s_m[c % 2], 16 * NH * (c // 2))
                    nc.vector.tensor_scalar_mul(mrow[:, c % 2, :], bank[0:NH * TPC, 0:P], -1.0).then_inc(s_free, 1)
                elif kind == "qa":
                    dve.wait_ge(s_cs[c % 2], 32 * (c // 2 + 1))
                    if c:
                        dve.wait_ge(s_hl, 4 * c)
                    nc.vector.tensor_tensor(ta, bank, cs[:, c % 2, 0, :], ALU.mult).then_inc(s_free, 1)
                elif kind == "qb":
                    nc.vector.tensor_tensor(tb, bank, cs[:, c % 2, 1, :], ALU.mult).then_inc(s_free, 1)
                    dve.wait_ge(s_free, n + 1)
                    done(nc.vector.tensor_tensor(ta, ta, tb, ALU.add))
                    settle()
                    if c:
                        dve.wait_ge(s_stk[(c - 1) % 2], 16 * 18 * ((c + 1) // 2))
                    nc.vector.tensor_copy(hl[:, 0, 0, :], ta).then_inc(s_hl, 1)
                    dve.wait_ge(s_hl, 4 * c + 1)
                    nc.vector.tensor_tensor(hl[:, 0, 1, :], ta, hl[:, 0, 0, :].bitcast(fp32),
                                            ALU.subtract).then_inc(s_hl, 1)
                elif kind == "kk":
                    H = NKV * HD
                    dve.wait_ge(s_hl, 4 * c + 2)
                    done(nc.vector.tensor_tensor(ta[0:H, :], bank[0:H, :], cs[0:H, c % 2, 0, :], ALU.mult))
                    nc.vector.tensor_tensor(tb[0:H, :], bank[H:2 * H, :], cs[H:2 * H, c % 2, 1, :], ALU.mult).then_inc(s_free, 1)
                    settle()
                    dve.wait_ge(s_free, n + 1)
                    done(nc.vector.tensor_tensor(ta[0:H, :], ta[0:H, :], tb[0:H, :], ALU.add))
                    settle()
                    nc.vector.tensor_copy(hl[0:H, 1, 0, :], ta[0:H, :]).then_inc(s_hl, 1)
                    dve.wait_ge(s_hl, 4 * c + 3)
                    nc.vector.tensor_tensor(hl[0:H, 1, 1, :], ta[0:H, :], hl[0:H, 1, 0, :].bitcast(fp32),
                                            ALU.subtract).then_inc(s_hl, 1)
                elif kind in ("to0", "to1"):
                    pair = int(kind == "to1")
                    four = bank.rearrange("p (t j a d) -> p t j a d", t=TPC, j=2, a=2)
                    done(nc.vector.reciprocal(rd[:, pair, :, :], four[:, :, :, 1, 0]))
                    settle()
                    nc.vector.tensor_tensor(yn[:, :, 2 * pair:2 * pair + 2, :], four[:, :, :, 0, :],
                                            rd[:, pair, :, :].unsqueeze(3).broadcast_to([P, TPC, 2, HD]),
                                            ALU.mult).then_inc(s_free, 1)
                elif kind == "ty":
                    nc.vector.tensor_copy(yT[:, :], bank).then_inc(s_free, 1)
                elif kind == "v":
                    nc.vector.tensor_copy(v1[:, TPC * c:TPC * c + TPC, :, 0:HD],
                                          bank[:, 0:TPC * NKV * HD].rearrange("p (t k d) -> p t k d", t=TPC, k=NKV)).then_inc(s_free, 1)
                elif kind == "wo":
                    nc.vector.tensor_tensor(xc, xc, bank.rearrange("p (t c) -> p t c", c=C), ALU.add).then_inc(s_free, 1)
                    dve.wait_ge(s_free, n + 1)
                    if c:
                        dve.wait_ge(s_item, ITEM[("ft", c - 1)] + 1)
                    done(nc.vector.tensor_tensor(sqa[:, :, :], xc, xc, ALU.mult))
                elif kind == "ft":
                    nc.vector.tensor_scalar(yT[:, :], bank, ln2s[:, 0:1], None, ALU.mult).then_inc(s_free, 1)
                elif kind == "rt":
                    nc.vector.tensor_copy(lg[:, :, :], bank[:, 0:TPC * NE].rearrange("p (t e) -> p t e", e=NE)).then_inc(s_free, 1)
                    dve.wait_ge(s_free, n + 1)
                    done(nc.vector.reduce_max(small4[:, 0, :], lg[:, :, :], X_AXIS))
                    settle()
                    nc.vector.tensor_tensor(lg[:, :, :], lg[:, :, :], over(small4[:, 0, :]), ALU.subtract).then_inc(s_rm, 1)
                elif kind == "cu":
                    done(nc.vector.tensor_tensor(place[:, :, :], bank[:, 0:TPC * NE].rearrange("p (t e) -> p t e", e=NE),
                                                 run[:, :].unsqueeze(1).broadcast_to([P, TPC, NE]), ALU.add))
                    settle()
                    nc.vector.tensor_tensor(run[:, :], run[:, :], bank[:, TPC * NE:TPC * NE + NE], ALU.add).then_inc(s_free, 1)
                    done(nc.vector.tensor_tensor(share[:, :, :, :], first[:, :, :, :],
                                                 place[:, :, :].unsqueeze(1).broadcast_to([P, 2, TPC, NE]), ALU.mult))
                    settle()
                    done(nc.vector.reduce_sum(two[:, :, :], share[:, :, :, :], X_AXIS))
                    settle()
                    nc.vector.tensor_copy(slot[:, :, :], two[:, :, :]).then_inc(s_slot, 1)

            dve.wait_ge(s_free, len(ITEM))
            thresholds = tiles[:, 0:N // P].unsqueeze(1).broadcast_to([1, NE, N // P])
            number = tiles[:, N // P:N // P + NT].unsqueeze(2).broadcast_to([1, NT, NR])
            starts = tiles[:, N // P + NT:N // P + NT + NR]
            expert = tiles[:, N // P + NT + NR:N // P + NT + 2 * NR].unsqueeze(1).broadcast_to([1, NT, NR])

            def per_tile(a):
                return a.unsqueeze(1).broadcast_to([1, NT, NR])

            nc.vector.tensor_copy(ends[:, :], run[0:1, :]).then_inc(s_tab, 1)
            done(nc.vector.tensor_tensor(tb2[:, 0, 0:NE], run[0:1, :], base[0:1, :], ALU.subtract))
            done(nc.vector.memset(tb2[:, 4, NE:NR], 2.0 * NT))
            settle()
            past = tb1[:, 0, :, :].rearrange("a n e -> a (n e)")[:, 0:NE * (N // P)].rearrange("a (e k) -> a e k", e=NE)
            done(nc.vector.tensor_tensor(past, tb2[:, 0, 0:NE].unsqueeze(2).broadcast_to([1, NE, N // P]), thresholds, ALU.is_gt))
            settle()
            done(nc.vector.reduce_sum(tb2[:, 1, 0:NE], past, X_AXIS))
            settle()
            for n, shift in enumerate((1, 2, 4)):
                done(nc.vector.tensor_copy(tb2[:, 2 + n, 0:shift], tb2[:, 1 + n, 0:shift]))
                done(nc.vector.tensor_tensor(tb2[:, 2 + n, shift:NE], tb2[:, 1 + n, shift:NE],
                                             tb2[:, 1 + n, 0:NE - shift], ALU.add))
                settle()
            done(nc.vector.tensor_tensor(tb2[:, 5, 0:NE], tb2[:, 4, 0:NE], tb2[:, 1, 0:NE], ALU.subtract))
            done(nc.vector.tensor_copy(tb2[:, 5, NE:NR], tb2[:, 4, NE - 1:NE]))
            settle()
            done(nc.vector.tensor_tensor(tb1[:, 0, :, :], number, per_tile(tb2[:, 4, :]), ALU.is_lt))
            done(nc.vector.tensor_tensor(tb1[:, 1, :, :], number, per_tile(tb2[:, 5, :]), ALU.is_ge))
            done(nc.vector.scalar_tensor_tensor(tb2[:, 0, :], tb2[:, 5, :], -float(P), starts, ALU.mult, ALU.add))
            done(nc.vector.tensor_scalar(tb1[:, 2, :, :], number, float(P), None, ALU.mult))
            settle()
            done(nc.vector.tensor_tensor(tb1[:, 0, :, :], tb1[:, 0, :, :], tb1[:, 1, :, :], ALU.mult))
            done(nc.vector.tensor_tensor(tb1[:, 2, :, :], tb1[:, 2, :, :], per_tile(tb2[:, 0, :]), ALU.add))
            settle()
            done(nc.vector.tensor_tensor(tb1[:, 1, :, :], tb1[:, 0, :, :], expert, ALU.mult))
            done(nc.vector.tensor_tensor(tb1[:, 2, :, :], tb1[:, 2, :, :], tb1[:, 0, :, :], ALU.mult))
            settle()
            done(nc.vector.reduce_sum(tb3[:, 0, :], tb1[:, 1, :, :], X_AXIS))
            done(nc.vector.reduce_sum(tb3[:, 1, :], tb1[:, 2, :, :], X_AXIS))
            settle()
            nc.vector.tensor_copy(table[:, :, :], tb3[:, :, :]).then_inc(s_tab, 1)
            nc.vector.tensor_tensor(xs[:, :, :], xs[:, :, :], us[:, :, :], ALU.add).then_inc(s_base, 1)

            def step(i, k, hidden=True, turned=True, result=True):
                s = XB * i + k
                later = not isinstance(i, int) or i > 0
                if hidden:
                    dve.wait_ge(s_sil, s + 1)
                    if k >= 2 or later:
                        dve.wait_ge(s_hp, s - 1)
                    nc.vector.tensor_tensor(hh[:, k % 2, :], sil[:, k % 2, :], ps[:, 3 + 2 * (k % 2), 0:HID],
                                            ALU.mult).then_inc(s_hh, 1)
                if turned:
                    dve.wait_ge(s_hp, s)
                    if k >= 3 or later:
                        dve.wait_ge(s_dn, s - 2)
                    b = (k - 1) % 2
                    nc.vector.tensor_copy(hhT[:, b, 0:2, :], ps[:, 6, 0:2 * P].rearrange("p (k c) -> p k c", c=P)).then_inc(s_hs, 1)
                    n = KB[2][1]
                    nc.vector.tensor_copy(hhT[0:n, b, 2, :], ps[0:n, 6, 2 * P:3 * P]).then_inc(s_hs, 1)
                if result:
                    dve.wait_ge(s_dn, s - 1)
                    kk = (k - 2) % XB
                    if k - 2 >= YB or later:
                        turn = XB // YB * (i if k >= 2 else i - 1) + kk // YB
                        dve.wait_ge(s_res[kk % YB], 16 * turn)
                    nc.vector.tensor_scalar(yo[:, kk % YB, :], ps[:, 7, 0:C], xt[:, kk, C:C + 1], None,
                                            ALU.mult).then_inc(s_yo, 1)

            for k in range(XB):
                step(0, k, turned=k >= 1, result=k >= 2)
            with dve.Fori(1, NT // XB) as i:
                for k in range(XB):
                    step(i, k)
            step(NT // XB, 0, hidden=False)
            step(NT // XB, 1, hidden=False, turned=False)

            for c in range(NCH):
                xc = xs[:, TPC * c:TPC * c + TPC, :]
                if c == 0:
                    dve.wait_ge(s_base, 1)
                dve.wait_ge(s_fin[c % 2], 16 * (c // 2 + 1))
                for r in range(2):
                    if r:
                        dve.wait_ge(s_sum, 2 * c + 1)
                    nc.vector.tensor_tensor(xc, xc, fin[:, c % 2, :, r, :], ALU.add).then_inc(s_sum, 1)

        @block.tensor
        def _(pe):
            def transposes(bank, src):
                for t in range(TPC):
                    last = nc.tensor.transpose(ps[:, bank, P * t:P * t + P], src(t), ident[:, :])
                return last

            def aggregate(ic, jg):
                pe.wait_ge(s_adj[jg % RING], adj_count(ic, jg))
                if jg == 0 and ic >= 2:
                    pe.wait_ge(s_aggT, ic - 1)
                for q in range(GRP):
                    j = GRP * jg + q
                    last = nc.tensor.matmul(ps[:, ic % 2, :], gs[:, j, :], ring[:, jg % RING, q, :],
                                            start=(j == 0), stop=(j == TILES - 1))
                last.then_inc(s_adj_pe, 1)

            pe.wait_ge(s_w, 64)
            pe.wait_ge(s_one, 1)
            nc.tensor.matmul(ps[:, 2, 0:P], wn[:, :], w2l[:, :], start=True, stop=True).then_inc(s_wgp, 1)
            for c in range(NCH + 2):
                if c < NCH:
                    pe.wait_ge(s_xn, c + 1)
                    if c >= 2:
                        pe.wait_ge(s_xnT, c - 1)
                    if c == 0:
                        pe.wait_ge(s_wg, 1)
                    transposes(2 + c % 2, lambda t: nrm[:, c % 2, t, :]).then_inc(s_xt, 1)
                if 1 <= c <= NCH:
                    d = c - 1
                    pe.wait_ge(s_xnT, d + 1)
                    if d >= 2:
                        pe.wait_ge(s_z, d - 1)
                    for t in range(TPC):
                        bank = 4 + 2 * (d % 2) + t // 2
                        last = nc.tensor.matmul(ps[:, bank, 2 * P * (t % 2):2 * P * (t % 2) + 2 * P],
                                                xnT[:, d % 2, P * t:P * t + P], wg[:, :, :],
                                                start=True, stop=True)
                    last.then_inc(s_gz, 1)
                if 2 <= c:
                    pe.wait_ge(s_g, c - 1)
                    aggregate(0, c - 2)

            def degree(ic):
                pe.wait_ge(s_fold, 3 * ic + 3)
                if ic:
                    pe.wait_ge(s_rdeg, 2 * ic - 1)
                nc.tensor.matmul(ps[:, 2, :], ones[:, :], acc_v[:, 0, :], start=True, stop=True).then_inc(s_deg, 1)

            def natural(ic):
                pe.wait_ge(s_aggT, ic + 1)
                if ic:
                    pe.wait_ge(s_x1, ic)
                transposes(3, lambda t: aggT[:, P * t:P * t + P]).then_inc(s_nat, 1)

            def h_rows(ic):
                pe.wait_ge(s_hn, ic + 1)
                if ic:
                    pe.wait_ge(s_hT, ic)
                transposes(4, lambda t: nrm[:, 0, t, :]).then_inc(s_ht, 1)

            pe.wait_ge(s_z, NCH)
            for ic in range(1, NCH):
                for jg in range(NGRP):
                    aggregate(ic, jg)
                    if jg == 0:
                        pass
                    if jg == 1:
                        degree(ic - 1)
                    if jg == 3:
                        natural(ic - 1)
                    if jg == 6:
                        h_rows(ic - 1)
            degree(NCH - 1)
            natural(NCH - 1)
            h_rows(NCH - 1)

            pe.wait_ge(s_c, 9 * 16)
            pe.wait_ge(s_mb, 2)
            pe.wait_ge(s_fill, 2)
            identb = maskb[:, 2, :]

            def values(u, c, st_, pair):
                pe.wait_ge(s_exp, 2 * u + 2)
                if st_ == 0 and c:
                    pe.wait_ge(s_y, c)
                pe.wait_ge(s_free, ITEM[("v", st_ // TPC)] + 1)
                lo = max(0, P * (st_ - TPC * c))
                for j in range(2):
                    last = nc.tensor.matmul(ps[2 * HD * j:2 * HD * j + 2 * HD, SB + pair, lo:CH],
                                            v1[:, st_, pair, :], pb[:, u % PB, j, lo:CH],
                                            start=(st_ == 0), stop=(st_ == TPC * (c + 1) - 1))
                last.then_inc(s_pv, 1)

            u = 0
            done_units = 0
            for o in ORDER:
                kind, c = o[0], o[1]
                if kind == "unit":
                    _, _, st_, pair = o
                    if st_ == 0 and pair == 0:
                        pe.wait_ge(s_m[c % 2], 16 * NH * (c // 2 + 1))
                    lo = max(0, P * (st_ - TPC * c))
                    diagonal = st_ >= TPC * c
                    for j in range(2):
                        h = 2 * pair + j
                        if 2 * u + j >= SB:
                            pe.wait_ge(s_exp, 2 * u + j - SB + 1)
                        o_ps = ps[:, (2 * u + j) % SB, :]
                        last = nc.tensor.matmul(o_ps[:, lo:CH], kst[0:MROW + 1, pair, P * st_:P * st_ + P],
                                                qst[0:MROW + 1, c % QS, h, lo:CH],
                                                start=True, stop=not diagonal)
                        if diagonal:
                            last = nc.tensor.matmul(o_ps[:, lo:lo + P], identb, maskb[:, 1, :],
                                                    start=False, stop=True)
                        last.then_inc(s_qk, 1)
                    u += 1
                    continue
                if kind == "values":
                    values(done_units, *o[1:])
                    done_units += 1
                if kind in ("values", "sum", "rx"):
                    continue
                n = ITEM[o]
                bank = ps[:, SB + 2 + n % IB, :]
                if n >= IB:
                    pe.wait_ge(s_free, n - IB + 1)
                if kind == "max":
                    _, _, t, h, k = o
                    if t == h == k == 0:
                        pe.wait_ge(s_stk[c % 2], 16 * 18 * (c // 2 + 1))
                    w = CH if k < c else P * (t + 1)
                    last = nc.tensor.matmul(bank[:, 0:w], qst[0:STACK, c % QS, h, P * t:P * t + P],
                                            kst[0:STACK, h // 2, CH * k:CH * k + w],
                                            start=True, stop=(k < c))
                    if k == c:
                        last = nc.tensor.matmul(bank[:, w - P:w], identb, maskb[:, 0, :], start=False, stop=True)
                elif kind == "mt":
                    pe.wait_ge(s_mred, c + 1)
                    last = nc.tensor.matmul(bank[0:NH * TPC, 0:P], mred[:, :], ident[:, :], start=True, stop=True)
                elif kind in ("qa", "qb"):
                    pe.wait_ge(s_hT, NCH)
                    last = nc.tensor.matmul(bank, wqs[:, int(kind == "qb"), :], hT[:, CH * c:CH * c + CH],
                                            start=True, stop=True)
                elif kind == "kk":
                    last = nc.tensor.matmul(bank, wks[:, :], hT[:, CH * c:CH * c + CH], start=True, stop=True)
                elif kind == "v":
                    for t in range(TPC):
                        r = CH * c + P * t
                        last = nc.tensor.matmul(bank[:, NKV * HD * t:NKV * HD * (t + 1)], hT[:, r:r + P], wvs[:, :],
                                                start=True, stop=True)
                elif kind in ("to0", "to1"):
                    pe.wait_ge(s_y, c + 1)
                    for t in range(TPC):
                        last = nc.tensor.transpose(bank[:, P * t:P * t + P], od[:, int(kind == "to1"), P * t:P * t + P],
                                                   ident[:, :])
                elif kind == "ty":
                    pe.wait_ge(s_free, ITEM[("to1", c)] + 1)
                    for t in range(TPC):
                        last = nc.tensor.transpose(bank[:, P * t:P * t + P], sqa[:, t, :], ident[:, :])
                elif kind == "wo":
                    pe.wait_ge(s_free, ITEM[("ty", c)] + 1)
                    for t in range(TPC):
                        last = nc.tensor.matmul(bank[:, C * t:C * t + C], yT[:, P * t:P * t + P], wos[:, :],
                                                start=True, stop=True)
                elif kind == "ft":
                    pe.wait_ge(s_fn, c + 1)
                    for t in range(TPC):
                        last = nc.tensor.transpose(bank[:, P * t:P * t + P], pay[:, 0, t, 0:C], ident[:, :])
                elif kind == "cu":
                    pe.wait_ge(s_sel, c + 1)
                    W = TPC * NE
                    nc.tensor.matmul(bank[:, 0:W], beforeb[:, 0, :], chosen[:, :, :], start=True, stop=True)
                    for t in range(1, TPC):
                        nc.tensor.matmul(bank[:, NE * t:W], beforeb[:, 1, :], chosen[:, 0:TPC - t, :],
                                         start=False, stop=True, skip_group_check=True)
                    for t in range(TPC):
                        last = nc.tensor.matmul(bank[:, W:W + NE], beforeb[:, 1, :], chosen[:, t, :],
                                                start=False, stop=True, skip_group_check=True)
                elif kind == "rt":
                    pe.wait_ge(s_free, ITEM[("ft", c)] + 1)
                    for t in range(TPC):
                        last = nc.tensor.matmul(bank[:, NE * t:NE * t + NE], yT[:, P * t:P * t + P], rts[:, :],
                                                start=True, stop=True)
                last.then_inc(s_item, 1)

            pe.wait_ge(s_free, len(ITEM))
            pe.wait_ge(s_moe, 16 * 4)
            pe.wait_ge(s_y, NCH)
            pe.wait_ge(s_tab, 2)

            experts = [pe.alloc_register(f"expert{k}") for k in range(XB + 2)]

            def experts_of(i):
                if isinstance(i, int) and i == 0:
                    pe.load(experts[2:], table[0:1, 0, 0:XB])
                elif isinstance(i, int) and i == NT // XB:
                    pe.load(experts[0:2], table[0:1, 0, NT - 2:NT])
                else:
                    pe.load(experts, table[0:1, 0, bass.ds(XB * i - 2, XB + 2)])

            def turn_rows(i, k):
                pe.wait_ge(s_ld[k], 16 * (i + 1))
                if k >= 2 or not isinstance(i, int) or i:
                    pe.wait_ge(s_us, XB * i + k - 1)
                nc.tensor.transpose(ps[:, k % 2, 0:P], xt[:, k, 0:C], ident[:, :]).then_inc(s_ut, 1)

            def step(i, k, turn=True, up=True, hidden=True, down=True):
                s = XB * i + k
                later = not isinstance(i, int) or i > 0
                if up:
                    e = pe.snap(experts[k + 2], min_val=0, max_val=NE - 1)
                    pe.wait_ge(s_us, s + 1)
                    if k >= 2 or later:
                        pe.wait_ge(s_hh, s - 1)
                    for j in range(2):
                        last = nc.tensor.matmul(ps[:, 2 + 2 * (k % 2) + j, 0:HID], xtT[:, k % 2, :],
                                                w13[:, bass.ds(e, 1), HID * j:HID * j + HID], start=True, stop=True)
                    last.then_inc(s_up, 1)
                if turn:
                    turn_rows(*((i, k + 1) if k + 1 < XB else (i + 1, 0)))
                if hidden:
                    pe.wait_ge(s_hh, s)
                    if k >= 2 or later:
                        pe.wait_ge(s_hs, 2 * (s - 1))
                    for j, (o, n) in enumerate(KB):
                        last = nc.tensor.transpose(ps[0:n, 6, P * j:P * j + P], hh[:, (k - 1) % 2, o:o + n], ident[:, :])
                    last.then_inc(s_hp, 1)
                if down:
                    e = pe.snap(experts[k], min_val=0, max_val=NE - 1)
                    pe.wait_ge(s_hs, 2 * (s - 1))
                    if k >= 3 or later:
                        pe.wait_ge(s_yo, s - 2)
                    for j, (o, n) in enumerate(KB):
                        last = nc.tensor.matmul(ps[:, 7, 0:C], hhT[0:n, k % 2, j, :],
                                                w2s[0:n, bass.ds(e, 1), j, :],
                                                start=(j == 0), stop=(j == len(KB) - 1))
                    last.then_inc(s_dn, 1)

            turn_rows(0, 0)
            experts_of(0)
            for k in range(XB):
                step(0, k, hidden=k >= 1, down=k >= 2)
            with pe.Fori(1, NT // XB - 1) as i:
                experts_of(i)
                for k in range(XB):
                    step(i, k)
            experts_of(NT // XB - 1)
            for k in range(XB):
                step(NT // XB - 1, k, turn=k + 1 < XB)
            experts_of(NT // XB)
            step(NT // XB, 0, turn=False, up=False)
            step(NT // XB, 1, turn=False, up=False, hidden=False)


def kernel(**inputs):
    import concourse.bacc as bacc
    from concourse.bass_utils import run_bass_kernel_spmd

    a = {k: np.asarray(v) for k, v in inputs.items()}
    lin = a["L0_gnn_lin_W"]
    swapped = (np.arange(HD) + HD // 2) % HD
    wq, wk = a["L0_ffn_wq"], a["L0_ffn_wk"]
    wqr = wq.reshape(NH, HD, C)[:, swapped].reshape(NH * HD, C)
    wkr = wk.reshape(NKV, HD, C)[:, swapped].reshape(NKV * HD, C)
    inv_freq = 1.0 / 10000.0 ** (np.arange(0, HD, 2, dtype=np.float32) / HD)
    freqs = np.outer(np.arange(N, dtype=np.float32), inv_freq)
    emb = np.concatenate([freqs, freqs], axis=-1)
    sign = np.where(np.arange(HD) < HD // 2, -1, 1).astype(np.float32)
    cos = np.tile(np.cos(emb).T, (NH, 1)).astype(np.float32)
    sin = np.tile((np.sin(emb) * sign).T, (NH, 1)).astype(np.float32)
    later = np.where(np.arange(P)[:, None] > np.arange(P)[None, :], np.float32(-1e30), np.float32(0))
    lower = (np.arange(NE)[None, :] < np.arange(NE)[:, None]).astype(np.float32)
    row = np.arange(P)
    before = np.stack([row[:, None] < row[None, :], np.ones((P, P), bool)], axis=1).astype(np.float32)
    starts = np.arange(NR, dtype=np.float32) * REG
    token = np.arange(TILES)[None, None, :] * P + row[:, None, None]
    dest = (2 * token + np.arange(2)[None, :, None]).astype(np.int32)
    tile_constants = np.concatenate([np.arange(N // P) * P, np.arange(NT), starts, np.arange(NR) % NE]
                                    ).astype(np.float32).reshape(1, -1)
    pad = np.zeros((2 * NE, P, ROW), np.float32)
    pad.view(np.int32)[:, :, C + 1] = 2 * N + P * np.arange(2 * NE)[:, None] + row
    arrays = {
        "x": a["x"].reshape(TILES, P, C).transpose(1, 0, 2),
        "adj_t": a["adj"].reshape(NCH, CH, NGRP, GRP, P).transpose(0, 2, 4, 3, 1),
        "neigh_w": a["L0_gnn_neigh_W"],
        "lin1_t": lin[:, :C].T,
        "lin2_t": lin[:, C:].T,
        "ln1": a["L0_ffn_ln1_w"].reshape(C, 1),
        "ln2": a["L0_ffn_ln2_w"].reshape(C, 1),
        "wq_t": wq.T,
        "wqr_t": wqr.T,
        "wk_t": np.concatenate([wk.T, wkr.T], axis=1),
        "wv_t": a["L0_ffn_wv"].T,
        "wo_t": a["L0_ffn_wo"].T,
        "router_t": a["L0_ffn_router_w"].T,
        "tri_in": np.broadcast_to(lower, (P, NE, NE)),
        "w13_t": np.concatenate([a["L0_ffn_w1"].transpose(2, 0, 1), a["L0_ffn_w3"].transpose(2, 0, 1)], axis=2),
        "w2_t": a["L0_ffn_w2"].transpose(0, 2, 1),
        "cos_t": cos,
        "sin_t": sin,
        "ident_in": np.eye(P, dtype=np.float32),
        "mask_in": np.stack([later.T, later], axis=1),
        "before_in": before,
        "base_in": np.broadcast_to(starts[:NE], (P, NE)),
        "dest_in": dest,
        "tile_in": tile_constants,
        "pad_in": pad,
    }
    arrays = {k: np.ascontiguousarray(v) for k, v in arrays.items()}
    nc = bacc.Bacc("TRN2", target_bir_lowering=False, num_devices=1)
    args = [nc.dram_tensor(k, v.shape, mybir.dt.from_np(v.dtype), kind="ExternalInput").ap()
            for k, v in arrays.items()]
    out = nc.dram_tensor("out", (P, TILES, C), fp32, kind="ExternalOutput").ap()
    build(nc, *args, out)
    got = run_bass_kernel_spmd(nc, [arrays], core_ids=[0]).results[0]["out"]
    return np.ascontiguousarray(got.transpose(1, 0, 2)).reshape(N, C)
```

```python
import concourse.bass as bass
from concourse import mybir
from concourse.alu_op_type import AluOpType as ALU
from contextlib import ExitStack
import numpy as np

fp32 = mybir.dt.float32
fp32r = mybir.dt.float32r
bf16 = mybir.dt.bfloat16
ACT = mybir.ActivationFunctionType
X_AXIS = mybir.AxisListType.X

P = 128
N = 4096
C = 128
TILES = N // P
CH = 512
NCH = N // CH
TPC = CH // P
NH, NKV, HD = 4, 2, 32
NE, HID = 8, 341
WARM_START = (6, 7)
WARM_TAIL = {"to0": 4, "ty": 6, "wo": 4, "ft": 20, "rt": 2, "cu": 22, "experts": 46}
X_PARTS = [(0, 1), (1, 4), (4, 8)]
SPREAD = [54, 54, 51, 54, 54, 54, 54, 53]
BEGIN = [0, 8, 8, 8, 8, 6, 8, 0]
GAP = [0, 1, 1, 3, 2, 2, 2, 0]
LATER = [0, 20, 20, 12, 20, 20, 20, 0]
RING = 4
GRP = TPC
NGRP = TILES // GRP
POOL_GRPS = 6
POOL_ADDS = 2 * POOL_GRPS - 1
FOLDS = 2
QS = 3
PB = 4
SB = 3
IB = 3
SCALE = 1.0 / float(np.sqrt(np.float32(HD)))
STACK = 3 * HD
MROW = STACK
REG = N + P
ROW = C + 4
SMALL_BYTES = 8704
NT = 2 * TILES + NE
SPARE = NE * REG
NR = NE + 1
XB = 12
YB = 4
KB = [(0, 128), (128, 128), (256, 85)]


def build(nc, x, adj_t, neigh_w, lin1_t, lin2_t, ln1, ln2, wq_t, wqr_t, wk_t, wv_t, wo_t,
          router_t, tri_in, w13_t, w2_t, cos_t, sin_t, ident_in, mask_in, before_in, base_in, dest_in, tile_in, pad_in, out):
    ctx = ExitStack()
    with ctx:
        def sb(name, shape, dt=fp32):
            return ctx.enter_context(nc.sbuf_tensor(name, shape, dt))

        def sem(name):
            return ctx.enter_context(nc.semaphore(name))

        xs = sb("xs", [P, TILES, C])
        us = sb("us", [P, TILES, C])
        hT = sb("hT", [P, N])
        kst = sb("kst", [P, NKV, N], fp32r)
        v1 = sb("v1", [P, TILES, NKV, 2 * HD])
        ident = sb("ident", [P, P])
        masks = sb("masks", [P, 2, P])
        maskb = sb("maskb", [P, 3, P], bf16)
        ln1s = sb("ln1s", [P, 1])
        ln2s = sb("ln2s", [P, 1])
        eps5 = sb("eps5", [P, 1])
        eps6 = sb("eps6", [P, 1])
        wqs = sb("wqs", [P, 2, P])
        wks = sb("wks", [P, P])
        wvs = sb("wvs", [P, NKV * HD])
        wos = sb("wos", [P, P])
        rts = sb("rts", [P, NE])
        ps = ctx.enter_context(nc.psum_tensor("ps", [P, 8, CH], fp32))

        gn = ExitStack()
        taken = [0]

        def gsb(name, shape, dt=fp32):
            taken[0] += 4 * int(np.prod(shape[1:]))
            return gn.enter_context(nc.sbuf_tensor(name, shape, dt))

        wn = gsb("wn", [P, P])
        w2l = gsb("w2l", [P, P])
        wg = gsb("wg", [P, 2, P])
        xnT = gsb("xnT", [P, 2, CH])
        twin = gsb("twin", [P, 3, TPC, C])
        first_end = taken[0]
        early_end = SMALL_BYTES + (8 + 2 * NH) * CH * 4
        gsb("gap", [P, (early_end - first_end) // 4])
        ring = gsb("ring", [P, RING, GRP, CH])
        gs = gsb("gs", [P, TILES, C])
        products_end = taken[0]
        acc_p = gsb("acc_p", [P, 2, CH])
        acc_v = gsb("acc_v", [P, 2, CH])
        ones = gsb("ones", [P, P])
        norm = gsb("norm", [P, 3, TPC, C])
        cen = [norm[:, 0], twin[:, 0]]
        nrm = [norm[:, 1], twin[:, 1]]
        sq = [norm[:, 2], twin[:, 2]]
        st = gsb("st", [P, 2, 8, TPC])
        deg = gsb("deg", [P, CH])
        aggT = nrm[0].rearrange("p t c -> p (t c)")

        s_x = [sem(f"x_loaded{c}") for c in range(len(X_PARTS))]
        s_warm = sem("table_loaded")
        s_w = sem("gnn_weights_loaded")
        s_c = sem("constants_loaded")
        s_adj = [sem(f"adj_loaded{r}") for r in range(RING)]
        s_adj_pe = sem("adj_multiplied")
        s_adj_pool = sem("adj_summed_pool")
        s_adj_dve = sem("adj_summed_dve")
        s_one = sem("ones_set")
        s_wgp = sem("wg_product")
        s_wg = sem("wg_ready")
        s_cen = sem("x_centred")
        s_sq = sem("squares")
        s_var = sem("variance_sum")
        s_std = sem("deviation")
        s_lnst = sem("ln_steps")
        s_xn = sem("x_normalised")
        s_xt = sem("xn_transposed")
        s_xnT = sem("xnT_ready")
        s_gz = sem("gz_product")
        s_g = sem("g_ready")
        s_z = sem("z_added")
        s_fold = sem("degree_fold")
        s_deg = sem("degree_product")
        s_rdeg = sem("degree_steps")
        s_aggT = sem("aggregate_scaled")
        s_nat = sem("aggregate_transposed")
        s_x1 = sem("x1_steps")
        s_u = sem("u_ready")
        s_usq = sem("u_squares")
        s_ustd = sem("u_deviation")
        s_hn = sem("h_normalised")
        s_ht = sem("h_transposed")
        s_hT = sem("hT_ready")
        s_out = sem("out_stored")
        gn.close()
        early = [0]

        def esb(name, shape, dt=fp32):
            size = int(np.prod(shape[1:])) * (2 if dt == bf16 else 4)
            early[0] += (size + 31) // 32 * 32
            return sb(name, shape, dt)

        mx = esb("mx", [P, NH * TPC, NCH])
        mred = esb("mred", [P, NH * TPC])
        mrow = esb("mrow", [NH * TPC, 2, P], fp32r)
        rec = esb("rec", [P, 2, CH])
        run = esb("run", [P, NE])
        tri = esb("tri", [P, NE, NE])
        beforef = esb("beforef", [P, 2, P])
        beforeb = esb("beforeb", [P, 2, P], bf16)
        base = esb("base", [P, NE])
        dest = esb("dest", [P, 2, TILES], mybir.dt.int32)
        W_TAB = N // P + 2 + NR + NR * NE + NR
        tiles = esb("tiles", [P, W_TAB])
        count = esb("count", [P, NR])
        pair_of = esb("pair_of", [P, 2, NR])
        assert early[0] <= SMALL_BYTES
        esb("fill", [P, (SMALL_BYTES - early[0]) // 4])
        with ExitStack() as over:
            cs = over.enter_context(nc.sbuf_tensor("cs", [P, 2, 2, CH], fp32))
            hl = over.enter_context(nc.sbuf_tensor("hl", [P, 2, 2, CH], fp32r))
            qst = over.enter_context(nc.sbuf_tensor("qst", [P, QS, NH, CH], fp32r))
        with ExitStack() as over:
            w13h = over.enter_context(nc.sbuf_tensor("w13h", [P, NE, 2 * HID], fp32r))
            xtT = over.enter_context(nc.sbuf_tensor("xtT", [P, 2, 2, P], fp32r))
        esb("front", [P, (4 + 4 + QS * NH) * CH])
        pb = sb("pb", [P, PB, 2, CH])
        ta, tb = rec[:, 0, :], rec[:, 1, :]
        yT = sb("yT", [P, CH])
        od = sb("od", [P, 2, CH])
        rd = sb("rd", [P, 2, TPC, 2])
        pay = sb("pay", [P, 2, TPC, ROW])
        sqa = sb("sqa", [P, TPC, C])
        yn = sqa[:, :, :].rearrange("p t (h d) -> p t h d", d=HD)
        warm = sb("warm", [P, 1])
        sta = sb("sta", [P, 4, TPC])
        lg = sb("lg", [P, TPC, NE])
        small4 = sb("small4", [P, 4, TPC])
        cmp = sb("cmp", [P, 2, TPC, NE, NE])
        rank = sb("rank", [P, TPC, NE])
        first = sb("first", [P, 2, TPC, NE])
        share = sb("share", [P, 2, TPC, NE])
        two = sb("two", [P, 2, TPC])
        chosen = sb("chosen", [P, TPC, NE], bf16)
        place = sb("place", [P, TPC, NE])
        slot = sb("slot", [P, 2, TPC], mybir.dt.int32)
        at = [N // P, N // P + 1, N // P + 2, N // P + 2 + NR, N // P + 2 + NR + NR * NE]
        thresholds = tiles[:, 0:at[0]]
        number, number_rows = tiles[:, at[0]:at[1]], tiles[:, at[1]:at[2]]
        starts = tiles[:, at[2]:at[3]]
        earlier_in = tiles[:, at[3]:at[4]].rearrange("p (a b) -> p a b", b=NE)
        experts_in = tiles[:, at[4]:W_TAB]
        rows = sb("rows", [P, NE])
        past = cmp[:, 0].rearrange("p t a b -> p (t a b)").rearrange("p (e k) -> p e k", e=NE)
        earlier = sb("earlier", [P, NR, NE])
        begin = sb("begin", [P, NR])
        finish = sb("finish", [P, NR])
        within = sb("within", [P, 2, NR])
        tile_row = sb("tile_row", [P, 2])
        table = sb("table", [1, 2, NT], mybir.dt.int32)
        ends = sb("ends", [1, NE], mybir.dt.int32)
        with ExitStack() as over:
            w13 = over.enter_context(nc.sbuf_tensor("w13", [P, NE, 2 * HID], fp32))
        w13l = sb("w13l", [P, NE, 2 * HID], fp32r)
        w2s = hT[:, 0:NE * len(KB) * C].rearrange("p (e k c) -> p e k c", e=NE, c=C)
        flat = pb[:, :, :, :].rearrange("p a b c -> p (a b c)")
        used = [0]

        def carve(*shape):
            n = int(np.prod(shape))
            view = flat[:, used[0]:used[0] + n]
            used[0] += n
            names = "abc"[:len(shape)]
            return view.rearrange("p (" + " ".join(names) + ") -> p " + " ".join(names),
                                  **dict(zip(names[1:], shape[1:])))

        xt = carve(XB, ROW)
        sil = carve(2, HID)
        hh = carve(2, HID)
        hhT = carve(2, len(KB), P)
        yo = od[:, 0, :].rearrange("p (b c) -> p b c", c=C)
        fin = kst[:, :, :].bitcast(fp32).rearrange("p k n -> p (k n)").rearrange(
            "p (b t r c) -> p b t r c", b=NCH, t=TPC, r=2)

        x_rows = nc.dram_tensor("dispatched_rows", [SPARE + NE * P, ROW], fp32, kind="Internal").ap()
        y_rows = nc.dram_tensor("result_rows", [2 * N + 2 * NE * P, C], fp32, kind="Internal").ap()

        s_cs = [sem(f"tables_loaded{b}") for b in range(2)]
        s_stk = [sem(f"stacks_filled{b}") for b in range(2)]
        s_m = [sem(f"maxima_placed{b}") for b in range(2)]
        s_moe = sem("expert_weights_loaded")
        s_mb = sem("masks_ready")
        s_fill = sem("ones_filled")
        s_item = sem("item_ready")
        s_free = [sem(f"item_read{b}") for b in range(IB)]
        s_vec = sem("vector_steps")
        s_hl = sem("split_ready")
        s_kt = sem("key_term_ready")
        s_rot = sem("rotated")
        s_mred = sem("maxima_reduced")
        s_qk = sem("scores_ready")
        s_exp = sem("probs_ready")
        s_pv = sem("values_added")
        s_y = sem("chunk_evacuated")
        s_y0 = sem("last_chunk_half_evacuated")
        s_sqa = sem("attention_squares")
        s_ss = sem("attention_squares_summed")
        s_sd = sem("attention_deviation")
        s_fn = sem("flat_normalised")
        s_rm = sem("router_shifted")
        s_re = sem("router_exp")
        s_rc = sem("router_constants_loaded")
        s_bb = sem("rows_zeroed")
        s_cp = sem("second_copy")
        s_sel = sem("experts_chosen")
        s_slot = sem("slots_ready")
        s_disp = sem("rows_dispatched")
        s_tab = sem("table_ready")
        s_tv = sem("table_values")
        s_tt = sem("table_turned")
        s_pad = sem("padding_stored")
        s_ld = [sem(f"tile_loaded{k}") for k in range(XB)]
        s_ut = sem("tile_transposed")
        s_us = sem("tile_scaled")
        s_ul = sem("tile_low_part")
        s_wh = sem("weights_high")
        s_wl = sem("weights_low")
        s_up = sem("up_products")
        s_sil = sem("silu_ready")
        s_hh = sem("hidden_ready")
        s_hp = sem("hidden_transposed")
        s_hs = sem("hiddenT_ready")
        s_dn = sem("down_products")
        s_yo = sem("result_ready")
        s_res = [sem(f"result_stored{k}") for k in range(YB)]
        s_fin = [sem(f"results_loaded{k}") for k in range(NCH)]
        s_sum = sem("results_added")
        s_base = sem("residuals_added")

        def units_before(c):
            return sum(2 * TPC * (k + 1) for k in range(c))

        NORM = ("n1", "n2", "n3", "n4", "hrow")
        AFTER = ("to0", "to1", "ty", "wo", "sum", "ft", "rt", "rx", "cu")
        BOTH = ("to0", "to1", "qa", "qb", "ty", "v", "wo", "sum", "kk", "ft", "rt", "rx", "cu")

        def items_of(c):
            def scores(c):
                return [("max", c, t, h, k) for t in range(TPC) for h in range(NH) for k in range(c + 1)]

            project = ("qa", "qb", "v", "kk")
            if c == -1:
                one = scores(1)
                return ([(k, n) for n in range(2) for k in project] + scores(0) + [("mt", 0)]
                        + one[:3] + [(k, 2) for k in project] + one[3:] + [("mt", 1)])
            if c == 0:
                return [("nat", NCH - 1)] + [(k, NCH - 1) for k in NORM]
            thin = [(k, c - 1) for k in AFTER]
            if c + 2 < NCH:
                thin = [(k, c + 2 if k in project else c - 1) for k in BOTH]
            if c + 1 >= NCH:
                return thin + [("weights", e) for e in range(NE)]
            among = scores(c + 1)
            for n, it in enumerate(thin):
                found_at = BEGIN[c] + (GAP[c] + 1) * n + (LATER[c] if it[0] == "cu" else 0)
                among.insert(min(found_at, len(among)), it)
            return among + [("mt", c + 1)]

        EARLY = {2: 4, 3: 12, 4: 12, 5: 12, 6: 12}
        n_early = sum(EARLY.values())
        first_items = items_of(-1)
        early_items = {}
        for ic in EARLY:
            upto = sum(EARLY[k] for k in EARLY if k <= ic)
            early_items[ic] = first_items[upto - EARLY[ic]:upto]

        ORDER = first_items[n_early:] + [("deg", NCH - 1)]
        last_unit = None
        for c in range(NCH):
            its = items_of(c)
            n_units = 2 * TPC * (c + 1)
            sent = 0
            steps = []
            for n in range(n_units):
                unit = (c, n // 2, n % 2)
                steps.append([("score",) + unit + (0,)])
                steps.append([("score",) + unit + (1,), ("unit",) + unit])
                if last_unit:
                    steps.append([("values",) + last_unit])
                last_unit = unit
            for n, some in enumerate(steps):
                ORDER += some
                upto = min(len(its), len(its) * (n + 1) * 64 // (len(steps) * SPREAD[c]))
                ORDER += its[sent:upto]
                sent = upto
        ORDER.append(("values",) + last_unit)
        ORDER += [(k, NCH - 1) for k in AFTER]
        ITEM = {}
        for o in first_items[:n_early] + ORDER:
            if o[0] not in ("unit", "score", "values", "sum", "rx", "weights") + NORM[:4]:
                ITEM[o] = len(ITEM)

        def split(eng, ops, c, k, H):
            if c:
                eng.wait_ge(s_stk[(c - 1) % 2], 16 * 18 * ((c + 1) // 2))
            ops.tensor_tensor(ta[0:H, :], ta[0:H, :], tb[0:H, :], ALU.add).then_inc(s_rot, 1)
            eng.wait_ge(s_rot, 2 * c + k + 1)
            ops.tensor_copy(hl[0:H, k, 0, :], ta[0:H, :]).then_inc(s_hl, 1)
            eng.wait_ge(s_hl, 4 * c + 2 * k + 1)
            ops.tensor_tensor(hl[0:H, k, 1, :], ta[0:H, :], hl[0:H, k, 0, :].bitcast(fp32),
                              ALU.subtract).then_inc(s_hl, 1)

        def item_bank(o):
            return ps[:, SB + 2 + ITEM[o] % IB, :]

        def free(o):
            return s_free[ITEM[o] % IB]

        def await_read(engine, o):
            engine.wait_ge(free(o), ITEM[o] // IB + 1)

        def await_all_read(engine):
            for b in range(IB):
                engine.wait_ge(s_free[b], (len(ITEM) - b + IB - 1) // IB)

        def adj_count(ic, jg):
            return 16 * (NGRP // RING * ic + jg // RING + 1)

        block = ctx.enter_context(nc.Block())

        @block.sync
        def _(sp):
            for k, (lo, hi) in enumerate(X_PARTS):
                sp.dma_start(xs[:, TPC * lo:TPC * hi, :], x[:, TPC * lo:TPC * hi, :]).then_inc(s_x[k], 16)
                if k == 0:
                    for dst, src in ((wn[:, :], neigh_w), (w2l[:, :], lin2_t), (wg[:, 1, :], lin1_t),
                                     (ident[:, :], ident_in)):
                        sp.dma_start(dst, src).then_inc(s_w, 16)

            def tables(c):
                if c >= 2:
                    await_read(sp, ("kk", c - 2))
                for k, src in enumerate((cos_t, sin_t)):
                    sp.dma_start(cs[:, c % 2, k, :], src[:, CH * c:CH * c + CH]).then_inc(s_cs[c % 2], 16)

            raw = hl[:, :, :, :].bitcast(fp32)

            def query_stack(c):
                sp.wait_ge(s_hl, 4 * c + 2)
                if c >= QS:
                    sp.wait_ge(s_qk, 2 * units_before(c - QS + 1))
                for h in range(NH):
                    for r, part in enumerate((0, 1, 0)):
                        sp.dma_start(qst[HD * r:HD * r + HD, c % QS, h, :].bitcast(fp32),
                                     raw[HD * h:HD * h + HD, 0, part, :]).then_inc(s_stk[c % 2], 16)

            def key_stack(c):
                sp.wait_ge(s_hl, 4 * c + 4)
                for h in range(NKV):
                    for r, part in enumerate((0, 0, 1)):
                        sp.dma_start(kst[HD * r:HD * r + HD, h, CH * c:CH * c + CH].bitcast(fp32),
                                     raw[HD * h:HD * h + HD, 1, part, :]).then_inc(s_stk[c % 2], 16)

            def stacks(c):
                query_stack(c)
                key_stack(c)

            def maxima(c):
                await_read(sp, ("mt", c))
                for h in range(NH):
                    sp.dma_start(qst[MROW:MROW + 1, c % QS, h, :].bitcast(fp32).rearrange("a (t c) -> a t c", c=P),
                                 mrow[TPC * h:TPC * h + TPC, c % 2, :].bitcast(fp32)).then_inc(s_m[c % 2], 16)
            for ic in range(NCH):
                if ic == 1:
                    for dst, src in ((masks[:, :, :], mask_in), (ln1s[:, :], ln1), (ln2s[:, :], ln2),
                                     (wqs[:, 0, :], wq_t), (wqs[:, 1, :], wqr_t), (wks[:, :], wk_t),
                                     (wvs[:, :], wv_t), (wos[:, :], wo_t), (rts[:, :], router_t)):
                        sp.dma_start(dst, src).then_inc(s_c, 16)
                if ic == 2:
                    sp.wait_ge(s_z, NCH)
                    tables(0)
                    tables(1)
                    for dst, src in ((tri[:, :, :], tri_in), (beforef[:, :, :], before_in), (base[:, :], base_in),
                                     (dest[:, :, :], dest_in), (tiles[:, :], tile_in)):
                        sp.dma_start(dst, src).then_inc(s_rc, 16)
                if ic == 4:
                    stacks(0)
                if ic == 5:
                    stacks(1)
                    tables(2)
                if ic == NCH - 1:
                    key_stack(2)
                if ic == 6:
                    maxima(0)
                for jg in range(NGRP):
                    if ic or jg >= RING:
                        ip, jp = (ic, jg - RING) if jg >= RING else (ic - 1, jg + NGRP - RING)
                        sp.wait_ge(s_adj_pe, NGRP * ip + jp + 1)
                        if jp < POOL_GRPS:
                            sp.wait_ge(s_adj_pool, POOL_ADDS * ip + 2 * jp + 1)
                        else:
                            sp.wait_ge(s_adj_dve, 3 * ip + (1 if jp == NGRP - 2 else 3))
                    sp.dma_start(ring[:, jg % RING, :, :], adj_t[ic, jg, :, :, :]).then_inc(s_adj[jg % RING], 16)
            sp.wait_ge(s_adj_pe, NGRP * NCH)
            sp.wait_ge(s_adj_pool, POOL_ADDS * NCH)
            sp.wait_ge(s_adj_dve, 3 * NCH)
            query_stack(2)
            maxima(1)
            sp.dma_start(x_rows[SPARE:SPARE + NE * P, :], pad_in[NE:2 * NE, :, :].rearrange("e p r -> (e p) r")).then_inc(s_pad, 16)
            for c in range(1, NCH - 1):
                if c + 2 < NCH:
                    tables(c + 2)
                    stacks(c + 2)
                maxima(c + 1)
                if c == 2:
                    await_read(sp, ("hrow", NCH - 1))
                    sp.dma_start(w13[:, :, :], w13_t).then_inc(s_moe, 16)
                if c + 2 == NCH - 1:
                    sp.wait_ge(s_item, ITEM[("kk", NCH - 1)] + 1)
                    for k, (o, n) in enumerate(KB):
                        sp.dma_start(w2s[0:n, :, k, :], w2_t[:, o:o + n, :].rearrange("e h c -> h e c")).then_inc(s_moe, 16)

            sp.wait_ge(s_tab, 1)
            end_rows = [sp.alloc_register(f"end_row{e}") for e in range(NE)]
            sp.load(end_rows, ends[0:1, :])
            for e in range(NE):
                end = sp.snap(end_rows[e], min_val=e * REG, max_val=e * REG + N)
                sp.dma_start(x_rows[bass.ds(end, P), :], pad_in[e, :, :]).then_inc(s_pad, 16)
            sp.wait_ge(s_tab, 2)
            sp.wait_ge(s_pad, 16 * (NE + 1))
            sp.wait_ge(s_disp, 16 * 2 * TILES)

            first_rows = [sp.alloc_register(f"first_row{k}") for k in range(XB)]

            def rows_of(i):
                sp.load(first_rows, table[0:1, 1, bass.ds(XB * i, XB)])

            def load(i, k):
                if not isinstance(i, int) or i:
                    sp.wait_ge(s_res[k % YB], 16 * (XB // YB * (i - 1) + k // YB + 1))
                row = sp.snap(first_rows[k], min_val=0, max_val=SPARE + (NE - 1) * P)
                sp.dma_start(xt[:, k, :], x_rows[bass.ds(row, P), :]).then_inc(s_ld[k], 16)

            rows_of(0)
            for k in range(XB):
                load(0, k)
            with sp.Fori(1, NT // XB) as i:
                rows_of(i)
                for k in range(XB):
                    load(i, k)
            for k in range(YB):
                sp.wait_ge(s_res[k], 16 * NT // YB)
            for c in range(NCH):
                sp.dma_start(fin[:, c], y_rows[2 * CH * c:2 * CH * c + 2 * CH, :].rearrange(
                    "(t p r) c -> p t r c", p=P, r=2)).then_inc(s_fin[c], 16)
            sp.wait_ge(s_out, 16 * NCH)

        @block.gpsimd
        def _(pool):
            nc.gpsimd.memset(kst[MROW:MROW + 1, :, :].bitcast(fp32), 1.0).then_inc(s_fill, 1)
            pool.wait_ge(s_fill, 1)
            nc.gpsimd.memset(v1[:, :, :, HD:2 * HD], 1.0).then_inc(s_fill, 1)
            for ic in range(NCH):
                for k in range(POOL_GRPS):
                    if ic == k == 0:
                        pool.wait_ge(s_fill, 2)
                    pool.wait_ge(s_adj[k % RING], adj_count(ic, k))
                    for half in range(1 if k == 0 else 2):
                        if k:
                            pool.wait_ge(s_adj_pool, POOL_ADDS * ic + 2 * k - 1 + half)
                        elif ic:
                            pool.wait_ge(s_fold, FOLDS * (ic - 1) + 1)
                        r = ring[:, k % RING, :, :]
                        a, b = (r[:, 0:2, :], r[:, 2:4, :]) if k == 0 else (acc_p[:, :, :], r[:, 2 * half:2 * half + 2, :])
                        nc.gpsimd.tensor_tensor(acc_p[:, :, :], a, b, ALU.add).then_inc(s_adj_pool, 1)

            for o in ORDER:
                kind, c = o[0], o[1]
                if kind == "qb" and c >= 3:
                    await_read(pool, ("qa", c))
                    await_read(pool, o)
                    split(pool, nc.gpsimd, c, 0, P)
                if kind == "kk" and c >= 3:
                    pool.wait_ge(s_kt, c + 1)
                    await_read(pool, o)
                    split(pool, nc.gpsimd, c, 1, NKV * HD)
                if kind != "cu":
                    continue
                pool.wait_ge(s_slot, c + 1)
                pool.wait_ge(s_cp, c + 1)
                for t in range(TPC):
                    for r in range(2):
                        pool.indirect_dma_start(
                            out=x_rows[:, :],
                            out_offset=bass.IndirectOffsetOnAxis(ap=slot[:, r, t:t + 1].bitcast(mybir.dt.uint32), axis=0),
                            in_=pay[:, r, t, :], in_offset=None).then_inc(s_disp, 16)

            def store(i, k):
                pool.wait_ge(s_yo, XB * i + k + 1)
                pool.indirect_dma_start(
                    out=y_rows[:, :],
                    out_offset=bass.IndirectOffsetOnAxis(ap=xt[:, k, C + 1:C + 2].bitcast(mybir.dt.uint32), axis=0),
                    in_=yo[:, k % YB, :], in_offset=None).then_inc(s_res[k % YB], 16)

            for i in range(NT // XB):
                for k in range(XB):
                    store(i, k)

        @block.scalar
        def _(act):
            act.wait_ge(s_one, 3)
            nc.scalar.activation(st[:, 0, 6, 0:1], eps5[:, :], ACT.Sqrt).then_inc(s_warm, 1)
            for c in range(NCH + 2):
                if c < NCH:
                    b = c % 2
                    act.wait_ge(s_cen, c + 1)
                    nc.scalar.activation(sq[b], cen[b], ACT.Square).then_inc(s_sq, 1)
                    if c == 0:
                        act.wait_ge(s_wgp, 1)
                        nc.scalar.copy(wg[:, 0, :], ps[:, 2, 0:P]).then_inc(s_wg, 1)
                    act.wait_ge(s_var, c + 1)
                    nc.scalar.activation(st[:, b, 3, :], st[:, b, 2, :], ACT.Sqrt, bias=eps5[:, 0:1],
                                         scale=1.0 / C).then_inc(s_std, 1)
                if 1 <= c <= NCH:
                    d = c - 1
                    act.wait_ge(s_xt, d + 1)
                    nc.scalar.copy(xnT[:, d % 2, :], ps[:, 2 + d % 2, :]).then_inc(s_xnT, 1)
                if 2 <= c:
                    d = c - 2
                    act.wait_ge(s_gz, d + 1)
                    bank = 4 + 2 * (d % 2)
                    gz = ps[:, bank:bank + 2, :].rearrange("p b (t s c) -> p (b t) s c", s=2, c=C)
                    nc.scalar.copy(gs[:, TPC * d:TPC * d + TPC, :], gz[:, :, 0, :]).then_inc(s_g, 1)
            act.wait_ge(s_c, 9 * 16)
            def norm_step(k, ic):
                if k == 0:
                    act.wait_ge(s_cen, NCH + ic + 1)
                    nc.scalar.activation(sq[0], cen[0], ACT.Square).then_inc(s_sq, 1)
                elif k == 1:
                    act.wait_ge(s_var, NCH + ic + 1)
                    nc.scalar.activation(st[:, 0, 3, :], st[:, 0, 2, :], ACT.Sqrt, bias=eps5[:, 0:1],
                                         scale=1.0 / C).then_inc(s_std, 1)
                elif k == 2:
                    act.wait_ge(s_u, 2 * ic + 1)
                    nc.scalar.activation(sq[0], us[:, TPC * ic:TPC * ic + TPC, :], ACT.Square).then_inc(s_usq, 1)
                else:
                    act.wait_ge(s_u, 2 * ic + 2)
                    nc.scalar.activation(st[:, 0, 6, :], st[:, 0, 5, :], ACT.Sqrt, bias=eps6[:, 0:1],
                                         scale=1.0 / C).then_inc(s_ustd, 1)

            def values_out(o):
                c = o[1]
                act.wait_ge(s_item, ITEM[o] + 1)
                nc.scalar.copy(v1[:, TPC * c:TPC * c + TPC, :, 0:HD],
                               item_bank(o)[:, 0:TPC * NKV * HD].rearrange("p (t k d) -> p t k d", t=TPC, k=NKV)
                               ).then_inc(free(o), 1)

            act.wait_ge(s_warm, 1)
            for ic in range(NCH - 1):
                for k in range(4):
                    norm_step(k, ic)
                act.wait_ge(s_ht, ic + 1)
                nc.scalar.activation(hT[:, CH * ic:CH * ic + CH], ps[:, 1, :], ACT.Copy,
                                     scale=ln1s[:, 0:1]).then_inc(s_hT, 1)
                for o in early_items.get(ic + 1, ()):
                    if o[0] == "v":
                        values_out(o)
            def evacuate(c):
                if c == NCH - 1:
                    act.wait_ge(s_pv, units_before(c + 1) - 1)
                    act.wait_ge(s_item, ITEM[("to1", c - 1)] + 1)
                    nc.scalar.copy(od[:, 0, :], ps[:, SB, :]).then_inc(s_y0, 1)
                    act.wait_ge(s_pv, units_before(c + 1))
                    nc.scalar.copy(od[:, 1, :], ps[:, SB + 1, :]).then_inc(s_y, 1)
                    return
                act.wait_ge(s_pv, units_before(c + 1))
                if c:
                    act.wait_ge(s_item, ITEM[("to1", c - 1)] + 1)
                nc.scalar.copy(od[:, :, :], ps[:, SB:SB + 2, :]).then_inc(s_y, 1)

            act.wait_ge(s_adj_pool, POOL_ADDS * NCH)
            act.wait_ge(s_adj_dve, 3 * NCH)
            u = 0
            for o in ORDER:
                if o[0] == "unit":
                    _, c, st_, pair = o
                    if u >= PB:
                        act.wait_ge(s_pv, u - PB + 1)
                    lo = max(0, P * (st_ - TPC * c))
                    for j in range(2):
                        act.wait_ge(s_qk, 2 * u + j + 1)
                        nc.scalar.activation(pb[:, u % PB, j, lo:CH], ps[:, (2 * u + j) % SB, lo:CH], ACT.Exp,
                                             scale=SCALE).then_inc(s_exp, 1)
                    u += 1
                    if c and (st_, pair) == (0, 0):
                        evacuate(c - 1)
                elif o[0] == "to0" and o[1] == NCH - 1:
                    evacuate(NCH - 1)
                    nc.scalar.activation(warm[:, 0:1], eps6[:, :], ACT.Sqrt).then_inc(s_warm, 1)
                elif o[0] == "v":
                    values_out(o)
                elif o[0] in NORM[:4]:
                    norm_step(NORM.index(o[0]), o[1])
                elif o[0] == "hrow":
                    act.wait_ge(s_item, ITEM[o] + 1)
                    nc.scalar.activation(hT[:, N - CH:N], item_bank(o), ACT.Copy, scale=ln1s[:, 0:1]).then_inc(free(o), 1)
                elif o[0] == "ty":
                    act.wait_ge(s_item, ITEM[o] + 1)
                    nc.scalar.copy(yT[:, :], item_bank(o)).then_inc(free(o), 1)
                elif o[0] == "sum":
                    c = o[1]
                    await_read(act, ("wo", c))
                    nc.scalar.activation(sqa[:, :, :], us[:, TPC * c:TPC * c + TPC, :], ACT.Square).then_inc(s_sqa, 1)
                elif o[0] == "ft":
                    act.wait_ge(s_ss, o[1] + 1)
                    nc.scalar.activation(sta[:, 1, :], sta[:, 0, :], ACT.Sqrt, bias=eps6[:, 0:1],
                                         scale=1.0 / C).then_inc(s_sd, 1)
                    act.wait_ge(s_item, ITEM[o] + 1)
                    nc.scalar.activation(yT[:, :], item_bank(o), ACT.Copy, scale=ln2s[:, 0:1]).then_inc(free(o), 1)
                elif o[0] == "rx":
                    c = o[1]
                    act.wait_ge(s_rm, c + 1)
                    nc.scalar.activation(lg[:, :, :], lg[:, :, :], ACT.Exp).then_inc(s_re, 1)
                    if c:
                        act.wait_ge(s_disp, 16 * 2 * TPC * c)
                    nc.scalar.copy(pay[:, 1, :, 0:C], pay[:, 0, :, 0:C]).then_inc(s_cp, 1)
            def step(i, k, scale=True, gate=True, turned=True):
                s = XB * i + k
                later = not isinstance(i, int) or i > 0
                if scale:
                    act.wait_ge(s_ut, s + 2)
                    if k >= 1 or not isinstance(i, int) or i:
                        act.wait_ge(s_up, s)
                    nc.scalar.activation(xtT[:, (k + 1) % 2, 0, :], ps[:, (k + 1) % 2, 0:P], ACT.Copy,
                                         scale=ln2s[:, 0:1]).then_inc(s_us, 1)
                if gate:
                    act.wait_ge(s_up, s + 1)
                    if k >= 2 or not isinstance(i, int) or i:
                        act.wait_ge(s_hh, s - 1)
                    nc.scalar.activation(sil[:, k % 2, :], ps[:, 2 + 2 * (k % 2), 0:HID], ACT.Silu).then_inc(s_sil, 1)
                if turned:
                    act.wait_ge(s_hp, s)
                    if k >= 3 or later:
                        act.wait_ge(s_dn, s - 2)
                    b = (k - 1) % 2
                    nc.scalar.copy(hhT[:, b, 0:2, :], ps[:, 6, 0:2 * P].rearrange("p (k c) -> p k c", c=P)).then_inc(s_hs, 1)
                    n = KB[2][1]
                    nc.scalar.copy(hhT[0:n, b, 2, :], ps[0:n, 6, 2 * P:3 * P]).then_inc(s_hs, 1)

            act.wait_ge(s_warm, 2)
            nc.scalar.activation(warm[:, 0:1], eps6[:, :], ACT.Silu).then_inc(s_warm, 1)
            act.wait_ge(s_ut, 1)
            nc.scalar.activation(xtT[:, 0, 0, :], ps[:, 0, 0:P], ACT.Copy, scale=ln2s[:, 0:1]).then_inc(s_us, 1)
            for k in range(XB):
                step(0, k, turned=k >= 1)
            with act.Fori(1, NT // XB - 1) as i:
                for k in range(XB):
                    step(i, k)
            for k in range(XB):
                step(NT // XB - 1, k, scale=k + 1 < XB)
            step(NT // XB, 0, scale=False, gate=False)
            for c in range(NCH):
                act.wait_ge(s_sum, 2 * c + 2)
                act.dma_start(out[:, TPC * c:TPC * c + TPC, :], xs[:, TPC * c:TPC * c + TPC, :]).then_inc(s_out, 16)

        @block.vector
        def _(dve):
            def wide(a):
                return a.unsqueeze(2).broadcast_to([P, TPC, C])

            nc.vector.memset(ones[:, :], 1.0).then_inc(s_one, 1)
            nc.vector.memset(eps5[:, :], 1e-5).then_inc(s_one, 1)
            nc.vector.memset(eps6[:, :], 1e-6).then_inc(s_one, 1)

            small = [0]

            def step(ins):
                small[0] += 1
                ins.then_inc(s_lnst, 1)
                dve.wait_ge(s_lnst, small[0])

            def centre(src, b):
                step(nc.vector.reduce_sum(st[:, b, 0, :], src, X_AXIS))
                step(nc.vector.tensor_scalar_mul(st[:, b, 1, :], st[:, b, 0, :], -1.0 / C))
                nc.vector.tensor_tensor(cen[b], src, wide(st[:, b, 1, :]), ALU.add).then_inc(s_cen, 1)

            def variance(n, b):
                dve.wait_ge(s_sq, n)
                nc.vector.reduce_sum(st[:, b, 2, :], sq[b], X_AXIS).then_inc(s_var, 1)

            def inverse(n, b):
                dve.wait_ge(s_std, n)
                step(nc.vector.reciprocal(st[:, b, 4, :], st[:, b, 3, :]))

            for c in range(NCH + 3):
                if c < NCH:
                    for k, (lo, _) in enumerate(X_PARTS):
                        if c == lo:
                            dve.wait_ge(s_x[k], 16)
                    centre(xs[:, TPC * c:TPC * c + TPC, :], c % 2)
                if 1 <= c <= NCH:
                    d, b = c - 1, (c - 1) % 2
                    inverse(d + 1, b)
                    if d >= 2:
                        dve.wait_ge(s_xt, d - 1)
                    nc.vector.tensor_tensor(nrm[b], cen[b], wide(st[:, b, 4, :]), ALU.mult).then_inc(s_xn, 1)
                if c < NCH:
                    variance(c + 1, c % 2)
                if 3 <= c:
                    d = c - 3
                    dve.wait_ge(s_g, d + 1)
                    bank = 4 + 2 * (d % 2)
                    gz = ps[:, bank:bank + 2, :].rearrange("p b (t s c) -> p (b t) s c", s=2, c=C)
                    xc = xs[:, TPC * d:TPC * d + TPC, :]
                    nc.vector.tensor_tensor(xc, xc, gz[:, :, 1, :], ALU.add).then_inc(s_z, 1)

            def fold(ic):
                dve.wait_ge(s_adj[6 % RING], adj_count(ic, 6))
                if ic:
                    dve.wait_ge(s_deg, ic)
                r = ring[:, 6 % RING, :, :]
                nc.vector.tensor_tensor(acc_v[:, :, :], r[:, 0:2, :], r[:, 2:4, :], ALU.add).then_inc(s_adj_dve, 1)
                dve.wait_ge(s_adj[7 % RING], adj_count(ic, 7))
                for half in range(2):
                    dve.wait_ge(s_adj_dve, 3 * ic + 1 + half)
                    nc.vector.tensor_tensor(acc_v[:, :, :], acc_v[:, :, :], ring[:, 7 % RING, 2 * half:2 * half + 2, :],
                                            ALU.add).then_inc(s_adj_dve, 1)
                dve.wait_ge(s_adj_dve, 3 * ic + 3)
                dve.wait_ge(s_adj_pool, POOL_ADDS * (ic + 1))
                nc.vector.tensor_tensor(acc_v[:, :, :], acc_v[:, :, :], acc_p[:, :, :], ALU.add).then_inc(s_fold, 1)
                dve.wait_ge(s_fold, FOLDS * ic + 1)
                nc.vector.tensor_tensor(acc_v[:, 0, :], acc_v[:, 0, :], acc_v[:, 1, :], ALU.add).then_inc(s_fold, 1)

            def mean(ic):
                if ic + 1 < NCH:
                    dve.wait_ge(s_deg, ic + 1)
                    nc.vector.tensor_scalar_add(deg[:, :], ps[:, 2, :], 1.0).then_inc(s_rdeg, 1)
                    dve.wait_ge(s_rdeg, 2 * ic + 1)
                    nc.vector.reciprocal(deg[:, :], deg[:, :]).then_inc(s_rdeg, 1)
                    dve.wait_ge(s_rdeg, 2 * ic + 2)
                else:
                    o = ("deg", ic)
                    nc.vector.tensor_scalar_add(deg[:, :], item_bank(o), 1.0).then_inc(free(o), 1)
                    await_read(dve, o)
                    nc.vector.reciprocal(deg[:, :], deg[:, :]).then_inc(s_rdeg, 1)
                    dve.wait_ge(s_rdeg, 2 * ic + 1)
                dve.wait_ge(s_adj_pe, NGRP * (ic + 1))
                if ic:
                    dve.wait_ge(s_nat, ic)
                    dve.wait_ge(s_ht, ic)
                nc.vector.tensor_tensor(aggT, ps[:, 4 * (ic % 2), :], deg[:, :], ALU.mult).then_inc(s_aggT, 1)

            def x1_step(ic):
                xc = xs[:, TPC * ic:TPC * ic + TPC, :]
                if ic + 1 < NCH:
                    dve.wait_ge(s_nat, ic + 1)
                    nc.vector.tensor_tensor(xc, xc, ps[:, 3, :].rearrange("p (t c) -> p t c", c=C),
                                            ALU.add).then_inc(s_x1, 1)
                    dve.wait_ge(s_x1, ic + 1)
                else:
                    o = ("nat", ic)
                    nc.vector.tensor_tensor(xc, xc, item_bank(o).rearrange("p (t c) -> p t c", c=C),
                                            ALU.add).then_inc(free(o), 1)
                    await_read(dve, o)
                centre(xc, 0)

            def norm_step(k, ic):
                uc = us[:, TPC * ic:TPC * ic + TPC, :]
                if k == 0:
                    variance(NCH + ic + 1, 0)
                elif k == 1:
                    inverse(NCH + ic + 1, 0)
                    nc.vector.tensor_tensor(uc, cen[0], wide(st[:, 0, 4, :]), ALU.mult).then_inc(s_u, 1)
                elif k == 2:
                    dve.wait_ge(s_usq, ic + 1)
                    nc.vector.reduce_sum(st[:, 0, 5, :], sq[0], X_AXIS).then_inc(s_u, 1)
                else:
                    dve.wait_ge(s_ustd, ic + 1)
                    step(nc.vector.reciprocal(st[:, 0, 7, :], st[:, 0, 6, :]))
                    nc.vector.tensor_tensor(nrm[0], uc, wide(st[:, 0, 7, :]), ALU.mult).then_inc(s_hn, 1)

            def after(ic):
                mean(ic)
                x1_step(ic)
                for k in range(4):
                    norm_step(k, ic)

            vec = [0]

            def done(ins):
                vec[0] += 1
                ins.then_inc(s_vec, 1)

            def settle():
                dve.wait_ge(s_vec, vec[0])

            routing = iter(())

            def over(a, n=NE):
                return a.unsqueeze(2).broadcast_to([P, TPC, n])

            def route(c):
                dve.wait_ge(s_re, c + 1)
                done(nc.vector.reduce_sum(small4[:, 1, :], lg[:, :, :], X_AXIS))
                yield
                settle()
                done(nc.vector.reciprocal(small4[:, 2, :], small4[:, 1, :]))
                yield
                settle()
                done(nc.vector.tensor_tensor(lg[:, :, :], lg[:, :, :], over(small4[:, 2, :]), ALU.mult))
                yield
                settle()
                other = lg[:, :, :].unsqueeze(2).broadcast_to([P, TPC, NE, NE])
                own = lg[:, :, :].unsqueeze(3).broadcast_to([P, TPC, NE, NE])
                lower = tri[:, :, :].unsqueeze(1).broadcast_to([P, TPC, NE, NE])
                done(nc.vector.tensor_tensor(cmp[:, 0], other, own, ALU.is_gt))
                done(nc.vector.tensor_tensor(cmp[:, 1], other, own, ALU.is_equal))
                yield
                settle()
                done(nc.vector.tensor_tensor(cmp[:, 1], cmp[:, 1], lower, ALU.mult))
                yield
                settle()
                done(nc.vector.tensor_tensor(cmp[:, 0], cmp[:, 0], cmp[:, 1], ALU.add))
                yield
                settle()
                done(nc.vector.reduce_sum(rank[:, :, :], cmp[:, 0], X_AXIS))
                yield
                settle()
                nc.vector.tensor_scalar(chosen[:, :, :], rank[:, :, :], 2.0, None, ALU.is_lt).then_inc(s_sel, 1)
                for r in range(2):
                    done(nc.vector.tensor_scalar(first[:, r], rank[:, :, :], float(r), None, ALU.is_equal))
                yield
                settle()
                done(nc.vector.tensor_tensor(share[:, :, :, :], first[:, :, :, :],
                                             lg[:, :, :].unsqueeze(1).broadcast_to([P, 2, TPC, NE]), ALU.mult))
                yield
                settle()
                done(nc.vector.reduce_sum(two[:, :, :], share[:, :, :, :], X_AXIS))
                yield
                settle()
                done(nc.vector.tensor_tensor(small4[:, 3, :], two[:, 0, :], two[:, 1, :], ALU.add))
                yield
                settle()
                done(nc.vector.tensor_scalar_add(small4[:, 3, :], small4[:, 3, :], 1e-9))
                yield
                settle()
                done(nc.vector.reciprocal(small4[:, 1, :], small4[:, 3, :]))
                yield
                settle()
                if c:
                    dve.wait_ge(s_disp, 16 * 2 * TPC * c)
                else:
                    dve.wait_ge(s_bb, 1)
                done(nc.vector.tensor_tensor(pay[:, :, :, C], two[:, :, :],
                                             small4[:, 1, :].unsqueeze(1).broadcast_to([P, 2, TPC]), ALU.mult))
                done(nc.vector.tensor_copy(pay[:, :, :, C + 1].bitcast(mybir.dt.int32),
                                           dest[:, :, TPC * c:TPC * c + TPC]))

            def constants():
                dve.wait_ge(s_c, 9 * 16)
                dve.wait_ge(s_w, 4 * 16)
                dve.wait_ge(s_rc, 5 * 16)
                done(nc.vector.tensor_copy(beforeb[:, :, :], beforef[:, :, :]))
                done(nc.vector.tensor_copy(run[:, :], base[:, :]))
                done(nc.vector.memset(count[:, NE:NR], 2.0 * NT))
                done(nc.vector.tensor_copy(pair_of[:, 0, :], experts_in))
                nc.vector.tensor_copy(maskb[:, 0:2, :], masks[:, :, :]).then_inc(s_mb, 1)
                nc.vector.tensor_copy(maskb[:, 2, :], ident[:, :]).then_inc(s_mb, 1)

            def item(o):
                nonlocal routing
                kind, c = o[0], o[1]
                if kind in ("unit", "score", "values"):
                    return
                if kind == "weights":
                    if c == 0:
                        dve.wait_ge(s_moe, 16)
                        dve.wait_ge(s_stk[1], 16 * 18 * (NCH // 2))
                        await_read(dve, ("kk", NCH - 1))
                        dve.wait_ge(s_qk, 2 * units_before(NCH - 1))
                    nc.vector.tensor_copy(w13h[:, c, :], w13[:, c, :]).then_inc(s_wh, 1)
                    dve.wait_ge(s_wh, c + 1)
                    nc.vector.tensor_tensor(w13l[:, c, :], w13[:, c, :], w13h[:, c, :].bitcast(fp32),
                                            ALU.subtract).then_inc(s_wl, 1)
                    return
                if kind in NORM:
                    if kind != "hrow":
                        norm_step(NORM.index(kind), c)
                    return
                xc = us[:, TPC * c:TPC * c + TPC, :]
                if kind == "sum":
                    dve.wait_ge(s_sqa, c + 1)
                    nc.vector.reduce_sum(sta[:, 0, :], sqa[:, :, :], X_AXIS).then_inc(s_ss, 1)
                    return
                if kind == "rx":
                    routing = route(c)
                    return
                if kind == "cu":
                    for _ in routing:
                        pass
                if kind == "ft":
                    dve.wait_ge(s_sd, c + 1)
                    done(nc.vector.reciprocal(sta[:, 2, :], sta[:, 1, :]))
                    settle()
                    if c:
                        dve.wait_ge(s_disp, 16 * 2 * TPC * c)
                    nc.vector.tensor_tensor(pay[:, 0, :, 0:C], xc, wide(sta[:, 2, :]), ALU.mult).then_inc(s_fn, 1)
                if kind == "mt":
                    for b in range(IB):
                        dve.wait_ge(s_free[b], (ITEM[o] - b + IB - 1) // IB)
                    nc.vector.reduce_max(mred[:, :], mx[:, :, 0:c + 1], X_AXIS).then_inc(s_mred, 1)
                if kind in ("ty", "v", "ft"):
                    return
                n = ITEM[o]
                bank = ps[:, SB + 2 + n % IB, :]
                dve.wait_ge(s_item, n + 1)
                if kind == "max":
                    _, _, t, h, k = o
                    w = CH if k < c else P * (t + 1)
                    if c and t == h == k == 0:
                        dve.wait_ge(s_mred, c)
                    nc.vector.reduce_max(mx[:, TPC * h + t, k:k + 1], bank[:, 0:w], X_AXIS).then_inc(free(o), 1)
                    next(routing, None)
                elif kind == "mt":
                    if c >= 2:
                        dve.wait_ge(s_m[c % 2], 16 * NH * (c // 2))
                    nc.vector.tensor_scalar_mul(mrow[:, c % 2, :], bank[0:NH * TPC, 0:P], -1.0).then_inc(free(o), 1)
                elif kind == "qa":
                    dve.wait_ge(s_cs[c % 2], 32 * (c // 2 + 1))
                    if c:
                        dve.wait_ge(s_hl, 4 * c)
                    nc.vector.tensor_tensor(ta, bank, cs[:, c % 2, 0, :], ALU.mult).then_inc(free(o), 1)
                elif kind == "qb":
                    nc.vector.tensor_tensor(tb, bank, cs[:, c % 2, 1, :], ALU.mult).then_inc(free(o), 1)
                    if c < 3:
                        await_read(dve, ("qa", c))
                        await_read(dve, o)
                        split(dve, nc.vector, c, 0, P)
                elif kind == "deg":
                    mean(c)
                elif kind == "nat":
                    x1_step(c)
                elif kind == "kk":
                    H = NKV * HD
                    dve.wait_ge(s_hl, 4 * c + 2)
                    nc.vector.tensor_tensor(ta[0:H, :], bank[0:H, :], cs[0:H, c % 2, 0, :], ALU.mult).then_inc(s_kt, 1)
                    nc.vector.tensor_tensor(tb[0:H, :], bank[H:2 * H, :], cs[H:2 * H, c % 2, 1, :], ALU.mult).then_inc(free(o), 1)
                    if c < 3:
                        dve.wait_ge(s_kt, c + 1)
                        await_read(dve, o)
                        split(dve, nc.vector, c, 1, H)
                elif kind in ("to0", "to1"):
                    pair = int(kind == "to1")
                    four = bank.rearrange("p (t j a d) -> p t j a d", t=TPC, j=2, a=2)
                    done(nc.vector.reciprocal(rd[:, pair, :, :], four[:, :, :, 1, 0]))
                    settle()
                    nc.vector.tensor_tensor(yn[:, :, 2 * pair:2 * pair + 2, :], four[:, :, :, 0, :],
                                            rd[:, pair, :, :].unsqueeze(3).broadcast_to([P, TPC, 2, HD]),
                                            ALU.mult).then_inc(free(o), 1)
                elif kind == "wo":
                    nc.vector.tensor_tensor(xc, xc, bank.rearrange("p (t c) -> p t c", c=C), ALU.add).then_inc(free(o), 1)
                elif kind == "rt":
                    nc.vector.tensor_copy(lg[:, :, :], bank[:, 0:TPC * NE].rearrange("p (t e) -> p t e", e=NE)).then_inc(free(o), 1)
                    await_read(dve, o)
                    done(nc.vector.reduce_max(small4[:, 0, :], lg[:, :, :], X_AXIS))
                    settle()
                    nc.vector.tensor_tensor(lg[:, :, :], lg[:, :, :], over(small4[:, 0, :]), ALU.subtract).then_inc(s_rm, 1)
                elif kind == "cu":
                    done(nc.vector.tensor_tensor(place[:, :, :], bank[:, 0:TPC * NE].rearrange("p (t e) -> p t e", e=NE),
                                                 run[:, :].unsqueeze(1).broadcast_to([P, TPC, NE]), ALU.add))
                    settle()
                    nc.vector.tensor_tensor(run[:, :], run[:, :], bank[:, TPC * NE:TPC * NE + NE], ALU.add).then_inc(free(o), 1)
                    done(nc.vector.tensor_tensor(share[:, :, :, :], first[:, :, :, :],
                                                 place[:, :, :].unsqueeze(1).broadcast_to([P, 2, TPC, NE]), ALU.mult))
                    settle()
                    done(nc.vector.reduce_sum(two[:, :, :], share[:, :, :, :], X_AXIS))
                    settle()
                    nc.vector.tensor_copy(slot[:, :, :], two[:, :, :]).then_inc(s_slot, 1)

            for ic in range(NCH):
                if ic:
                    after(ic - 1)
                if ic == 2:
                    constants()
                fold(ic)
                for o in early_items.get(ic, ()):
                    item(o)
            dve.wait_ge(s_adj_pe, NGRP * NCH)
            dve.wait_ge(s_adj_pool, POOL_ADDS * NCH)
            nc.vector.memset(pay[:, :, :, C:ROW], 0.0).then_inc(s_bb, 1)
            for o in ORDER:
                item(o)

            await_all_read(dve)
            nc.vector.tensor_copy(ends[:, :], run[0:1, :]).then_inc(s_tab, 1)
            done(nc.vector.tensor_tensor(rows[:, :], run[:, :], base[:, :], ALU.subtract))
            settle()
            done(nc.vector.tensor_tensor(past[:, :, :], rows[:, :].unsqueeze(2).broadcast_to([P, NE, N // P]),
                                         thresholds.unsqueeze(1).broadcast_to([P, NE, N // P]), ALU.is_gt))
            settle()
            done(nc.vector.reduce_sum(count[:, 0:NE], past[:, :, :], X_AXIS))
            settle()
            done(nc.vector.tensor_tensor(earlier[:, :, :], count[:, 0:NE].unsqueeze(1).broadcast_to([P, NR, NE]),
                                         earlier_in, ALU.mult))
            settle()
            done(nc.vector.reduce_sum(begin[:, :], earlier[:, :, :], X_AXIS))
            settle()
            done(nc.vector.tensor_tensor(finish[:, :], begin[:, :], count[:, :], ALU.add))
            done(nc.vector.tensor_scalar(within[:, 0, :], begin[:, :], number, None, ALU.is_le))
            done(nc.vector.scalar_tensor_tensor(pair_of[:, 1, :], begin[:, :], -float(P), starts, ALU.mult, ALU.add))
            settle()
            done(nc.vector.tensor_scalar(within[:, 1, :], finish[:, :], number, None, ALU.is_gt))
            done(nc.vector.tensor_scalar(pair_of[:, 1, :], pair_of[:, 1, :], number_rows, None, ALU.add))
            settle()
            done(nc.vector.tensor_tensor(within[:, 0, :], within[:, 0, :], within[:, 1, :], ALU.mult))
            settle()
            done(nc.vector.tensor_tensor(pair_of[:, :, :], pair_of[:, :, :],
                                         within[:, 0, :].unsqueeze(1).broadcast_to([P, 2, NR]), ALU.mult))
            settle()
            nc.vector.reduce_sum(tile_row[:, :], pair_of[:, :, :], X_AXIS).then_inc(s_tv, 1)
            dve.wait_ge(s_tt, 1)
            nc.vector.tensor_copy(table[:, :, :], ps[0:1, 0, 0:2 * NT].rearrange("p (a n) -> p a n", a=2)).then_inc(s_tab, 1)
            nc.vector.tensor_tensor(xs[:, :, :], xs[:, :, :], us[:, :, :], ALU.add).then_inc(s_base, 1)

            def low_part(s, k):
                dve.wait_ge(s_us, s + 1)
                nc.vector.scalar_tensor_tensor(xtT[:, k % 2, 1, :], ps[:, k % 2, 0:P], ln2s[:, 0:1],
                                               xtT[:, k % 2, 0, :].bitcast(fp32), ALU.mult, ALU.subtract).then_inc(s_ul, 1)

            def step(i, k, low=True, hidden=True, result=True):
                s = XB * i + k
                later = not isinstance(i, int) or i > 0
                if low:
                    low_part(s + 1, k + 1)
                if hidden:
                    dve.wait_ge(s_sil, s + 1)
                    if k >= 2 or later:
                        dve.wait_ge(s_hp, s - 1)
                    nc.vector.tensor_tensor(hh[:, k % 2, :], sil[:, k % 2, :], ps[:, 3 + 2 * (k % 2), 1:HID + 1],
                                            ALU.mult).then_inc(s_hh, 1)
                if result:
                    dve.wait_ge(s_dn, s - 1)
                    kk = (k - 2) % XB
                    if k - 2 >= YB or later:
                        turn = XB // YB * (i if k >= 2 else i - 1) + kk // YB
                        dve.wait_ge(s_res[kk % YB], 16 * turn)
                    nc.vector.tensor_scalar(yo[:, kk % YB, :], ps[:, 7, 0:C], xt[:, kk, C:C + 1], None,
                                            ALU.mult).then_inc(s_yo, 1)

            low_part(0, 0)
            for k in range(XB):
                step(0, k, result=k >= 2)
            with dve.Fori(1, NT // XB - 1) as i:
                for k in range(XB):
                    step(i, k)
            for k in range(XB):
                step(NT // XB - 1, k, low=k + 1 < XB)
            step(NT // XB, 0, low=False, hidden=False)
            step(NT // XB, 1, low=False, hidden=False)

            for c in range(NCH):
                xc = xs[:, TPC * c:TPC * c + TPC, :]
                if c == 0:
                    dve.wait_ge(s_base, 1)
                dve.wait_ge(s_fin[c], 16)
                for r in range(2):
                    if r:
                        dve.wait_ge(s_sum, 2 * c + 1)
                    nc.vector.tensor_tensor(xc, xc, fin[:, c, :, r, :], ALU.add).then_inc(s_sum, 1)

        @block.tensor
        def _(pe):
            def transposes(bank, src):
                for t in range(TPC):
                    last = nc.tensor.transpose(ps[:, bank, P * t:P * t + P], src(t), ident[:, :])
                return last

            def aggregate(ic, jg, among=()):
                pe.wait_ge(s_adj[jg % RING], adj_count(ic, jg))
                if jg == 0 and ic >= 2:
                    pe.wait_ge(s_aggT, ic - 1)
                for q in range(GRP):
                    j = GRP * jg + q
                    last = nc.tensor.matmul(ps[:, 4 * (ic % 2), :], gs[:, j, :], ring[:, jg % RING, q, :],
                                            start=(j == 0), stop=(j == TILES - 1))
                    if q == GRP - 1:
                        last.then_inc(s_adj_pe, 1)
                    for o in among[q:q + 1]:
                        item(o)

            def keep_warm(n, src, bank=0):
                for _ in range(n):
                    nc.tensor.matmul(ps[:, bank, 0:src.shape[-1]], src[:, 0:P], src, start=True, stop=True)

            pe.wait_ge(s_one, 1)
            keep_warm(WARM_START[0], ones[:, :])
            pe.wait_ge(s_w, 64)
            nc.tensor.matmul(ps[:, 2, 0:P], wn[:, :], w2l[:, :], start=True, stop=True).then_inc(s_wgp, 1)
            keep_warm(WARM_START[1], ones[:, :])
            for c in range(NCH + 2):
                if c < NCH:
                    pe.wait_ge(s_xn, c + 1)
                    if c >= 2:
                        pe.wait_ge(s_xnT, c - 1)
                    if c == 0:
                        pe.wait_ge(s_wg, 1)
                    transposes(2 + c % 2, lambda t: nrm[c % 2][:, t, :]).then_inc(s_xt, 1)
                if 1 <= c <= NCH:
                    d = c - 1
                    pe.wait_ge(s_xnT, d + 1)
                    if d >= 2:
                        pe.wait_ge(s_z, d - 1)
                    for t in range(TPC):
                        bank = 4 + 2 * (d % 2) + t // 2
                        last = nc.tensor.matmul(ps[:, bank, 2 * P * (t % 2):2 * P * (t % 2) + 2 * P],
                                                xnT[:, d % 2, P * t:P * t + P], wg[:, :, :],
                                                start=True, stop=True)
                    last.then_inc(s_gz, 1)
                if 2 <= c:
                    pe.wait_ge(s_g, c - 1)
                    aggregate(0, c - 2)

            def degree(ic):
                pe.wait_ge(s_fold, FOLDS * ic + 2)
                if ic:
                    pe.wait_ge(s_rdeg, 2 * ic - 1)
                nc.tensor.matmul(ps[:, 2, :], ones[:, :], acc_v[:, 0, :], start=True, stop=True).then_inc(s_deg, 1)

            def natural(ic):
                pe.wait_ge(s_aggT, ic + 1)
                if ic:
                    pe.wait_ge(s_x1, ic)
                transposes(3, lambda t: aggT[:, P * t:P * t + P]).then_inc(s_nat, 1)

            def h_rows(ic):
                pe.wait_ge(s_hn, ic + 1)
                if ic:
                    pe.wait_ge(s_hT, ic)
                transposes(1, lambda t: nrm[0][:, t, :]).then_inc(s_ht, 1)

            identb = maskb[:, 2, :]

            def values(u, c, st_, pair):
                pe.wait_ge(s_exp, 2 * u + 2)
                if u == 1:
                    pe.wait_ge(s_aggT, NCH)
                if st_ == 0 and c:
                    pe.wait_ge(s_y, c)
                await_read(pe, ("v", st_ // TPC))
                lo = max(0, P * (st_ - TPC * c))
                for j in range(2):
                    last = nc.tensor.matmul(ps[2 * HD * j:2 * HD * j + 2 * HD, SB + pair, lo:CH],
                                            v1[:, st_, pair, :], pb[:, u % PB, j, lo:CH],
                                            start=(st_ == 0), stop=(st_ == TPC * (c + 1) - 1))
                last.then_inc(s_pv, 1)

            def await_h(c):
                if c + 1 < NCH:
                    pe.wait_ge(s_hT, c + 1)
                else:
                    await_read(pe, ("hrow", c))

            def item(o):
                kind, c = o[0], o[1]
                n = ITEM[o]
                bank = ps[:, SB + 2 + n % IB, :]
                if n >= IB:
                    pe.wait_ge(s_free[n % IB], n // IB)
                if kind == "max":
                    _, _, t, h, k = o
                    if t == h == k == 0:
                        pe.wait_ge(s_stk[c % 2], 16 * 18 * (c // 2 + 1))
                    w = CH if k < c else P * (t + 1)
                    last = nc.tensor.matmul(bank[:, 0:w], qst[0:STACK, c % QS, h, P * t:P * t + P],
                                            kst[0:STACK, h // 2, CH * k:CH * k + w],
                                            start=True, stop=(k < c))
                    if k == c:
                        last = nc.tensor.matmul(bank[:, w - P:w], identb, maskb[:, 0, :], start=False, stop=True)
                elif kind == "mt":
                    pe.wait_ge(s_mred, c + 1)
                    last = nc.tensor.matmul(bank[0:NH * TPC, 0:P], mred[:, :], ident[:, :], start=True, stop=True)
                elif kind in ("qa", "qb"):
                    await_h(c)
                    last = nc.tensor.matmul(bank, wqs[:, int(kind == "qb"), :], hT[:, CH * c:CH * c + CH],
                                            start=True, stop=True)
                elif kind == "deg":
                    pe.wait_ge(s_fold, FOLDS * NCH)
                    last = nc.tensor.matmul(bank, ones[:, :], acc_v[:, 0, :], start=True, stop=True)
                elif kind in ("nat", "hrow"):
                    if kind == "nat":
                        pe.wait_ge(s_aggT, NCH)
                    else:
                        pe.wait_ge(s_hn, NCH)
                    for t in range(TPC):
                        src = aggT[:, P * t:P * t + P] if kind == "nat" else nrm[0][:, t, :]
                        last = nc.tensor.transpose(bank[:, P * t:P * t + P], src, ident[:, :])
                elif kind == "kk":
                    last = nc.tensor.matmul(bank, wks[:, :], hT[:, CH * c:CH * c + CH], start=True, stop=True)
                elif kind == "v":
                    for t in range(TPC):
                        r = CH * c + P * t
                        last = nc.tensor.matmul(bank[:, NKV * HD * t:NKV * HD * (t + 1)], hT[:, r:r + P], wvs[:, :],
                                                start=True, stop=True)
                elif kind in ("to0", "to1"):
                    if kind == "to0" and c == NCH - 1:
                        pe.wait_ge(s_y0, 1)
                    else:
                        pe.wait_ge(s_y, c + 1)
                    for t in range(TPC):
                        last = nc.tensor.transpose(bank[:, P * t:P * t + P], od[:, int(kind == "to1"), P * t:P * t + P],
                                                   ident[:, :])
                elif kind == "ty":
                    await_read(pe, ("to1", c))
                    for t in range(TPC):
                        last = nc.tensor.transpose(bank[:, P * t:P * t + P], sqa[:, t, :], ident[:, :])
                elif kind == "wo":
                    await_read(pe, ("ty", c))
                    for t in range(TPC):
                        last = nc.tensor.matmul(bank[:, C * t:C * t + C], yT[:, P * t:P * t + P], wos[:, :],
                                                start=True, stop=True)
                elif kind == "ft":
                    pe.wait_ge(s_fn, c + 1)
                    for t in range(TPC):
                        last = nc.tensor.transpose(bank[:, P * t:P * t + P], pay[:, 0, t, 0:C], ident[:, :])
                elif kind == "cu":
                    pe.wait_ge(s_sel, c + 1)
                    W = TPC * NE
                    nc.tensor.matmul(bank[:, 0:W], beforeb[:, 0, :], chosen[:, :, :], start=True, stop=True)
                    for t in range(1, TPC):
                        nc.tensor.matmul(bank[:, NE * t:W], beforeb[:, 1, :], chosen[:, 0:TPC - t, :],
                                         start=False, stop=True, skip_group_check=True)
                    for t in range(TPC):
                        last = nc.tensor.matmul(bank[:, W:W + NE], beforeb[:, 1, :], chosen[:, t, :],
                                                start=False, stop=True, skip_group_check=True)
                elif kind == "rt":
                    await_read(pe, ("ft", c))
                    for t in range(TPC):
                        last = nc.tensor.matmul(bank[:, NE * t:NE * t + NE], yT[:, P * t:P * t + P], rts[:, :],
                                                start=True, stop=True)
                last.then_inc(s_item, 1)

            pe.wait_ge(s_z, NCH)
            for ic in range(1, NCH):
                for jg in range(NGRP):
                    if ic == 2 and jg == NGRP - 1:
                        pe.wait_ge(s_c, 9 * 16)
                        pe.wait_ge(s_mb, 2)
                        pe.wait_ge(s_fill, 2)
                    if jg == NGRP - 1:
                        among = early_items.get(ic, ())[0:GRP]
                    else:
                        among = early_items.get(ic - 1, ())[GRP * (jg + 1):GRP * (jg + 2)]
                    aggregate(ic, jg, among)
                    if jg == 1:
                        degree(ic - 1)
                    if jg == 3:
                        natural(ic - 1)
                    if jg == 6:
                        h_rows(ic - 1)

            u = 0
            done_units = 0
            pe.wait_ge(s_hT, NCH - 1)
            for o in ORDER:
                kind, c = o[0], o[1]
                if kind == "score":
                    _, _, st_, pair, j = o
                    if st_ == pair == j == 0:
                        pe.wait_ge(s_m[c % 2], 16 * NH * (c // 2 + 1))
                    lo = max(0, P * (st_ - TPC * c))
                    diagonal = st_ >= TPC * c
                    if u >= SB:
                        pe.wait_ge(s_exp, u - SB + 1)
                    o_ps = ps[:, u % SB, :]
                    last = nc.tensor.matmul(o_ps[:, lo:CH], kst[0:MROW + 1, pair, P * st_:P * st_ + P],
                                            qst[0:MROW + 1, c % QS, 2 * pair + j, lo:CH], start=True, stop=not diagonal)
                    if diagonal:
                        last = nc.tensor.matmul(o_ps[:, lo:lo + P], identb, maskb[:, 1, :], start=False, stop=True)
                    last.then_inc(s_qk, 1)
                    u += 1
                    continue
                if kind == "values":
                    values(done_units, *o[1:])
                    done_units += 1
                elif o in ITEM:
                    if c == NCH - 1 and kind in WARM_TAIL:
                        keep_warm(WARM_TAIL[kind], maskb[:, :, :].rearrange("p a b -> p (a b)"))
                    item(o)
            await_all_read(pe)
            pe.wait_ge(s_moe, 16 * 4)
            pe.wait_ge(s_wl, NE)
            pe.wait_ge(s_y, NCH)
            pe.wait_ge(s_tv, 1)
            pe.wait_ge(s_exp, 2 * units_before(NCH))
            for k in range(2):
                last = nc.tensor.matmul(ps[0:1, 0, NT * k:NT * k + NT], tile_row[0:NT, k:k + 1], ident[0:NT, 0:NT],
                                        start=True, stop=True)
            last.then_inc(s_tt, 1)
            keep_warm(WARM_TAIL["experts"], maskb[:, :, :].rearrange("p a b -> p (a b)"), 1)
            pe.wait_ge(s_tab, 2)

            experts = [pe.alloc_register(f"expert{k}") for k in range(XB + 2)]

            def experts_of(i):
                if isinstance(i, int) and i == 0:
                    pe.load(experts[2:], table[0:1, 0, 0:XB])
                elif isinstance(i, int) and i == NT // XB:
                    pe.load(experts[0:2], table[0:1, 0, NT - 2:NT])
                else:
                    pe.load(experts, table[0:1, 0, bass.ds(XB * i - 2, XB + 2)])

            def turn_rows(i, k):
                pe.wait_ge(s_ld[k], 16 * (i + 1))
                if k >= 2 or not isinstance(i, int) or i:
                    pe.wait_ge(s_ul, XB * i + k - 1)
                nc.tensor.transpose(ps[:, k % 2, 0:P], xt[:, k, 0:C], ident[:, :]).then_inc(s_ut, 1)

            def step(i, k, turn=True, up=True, hidden=True, down=True):
                s = XB * i + k
                later = not isinstance(i, int) or i > 0
                if up:
                    e = pe.snap(experts[k + 2], min_val=0, max_val=NE - 1)
                    if k >= 2 or later:
                        pe.wait_ge(s_hh, s - 1)
                    parts = ((0, w13h), (0, w13l), (1, w13h))
                    for n, (part, w) in enumerate(parts):
                        if part == 0:
                            pe.wait_ge(s_us, s + 1)
                        else:
                            pe.wait_ge(s_ul, s + 1)
                        for j in range(2):
                            last = nc.tensor.matmul(ps[:, 2 + 2 * (k % 2) + j, 0:HID + 1], xtT[:, k % 2, part, :],
                                                    w[:, bass.ds(e, 1), (HID - 1) * j:(HID - 1) * j + HID + 1],
                                                    start=(n == 0), stop=(n == len(parts) - 1))
                    last.then_inc(s_up, 1)
                if turn:
                    turn_rows(*((i, k + 1) if k + 1 < XB else (i + 1, 0)))
                if hidden:
                    pe.wait_ge(s_hh, s)
                    if k >= 2 or later:
                        pe.wait_ge(s_hs, 2 * (s - 1))
                    for j, (o, n) in enumerate(KB):
                        last = nc.tensor.transpose(ps[0:n, 6, P * j:P * j + P], hh[:, (k - 1) % 2, o:o + n], ident[:, :])
                    last.then_inc(s_hp, 1)
                if down:
                    e = pe.snap(experts[k], min_val=0, max_val=NE - 1)
                    pe.wait_ge(s_hs, 2 * (s - 1))
                    if k >= 3 or later:
                        pe.wait_ge(s_yo, s - 2)
                    for j, (o, n) in enumerate(KB):
                        last = nc.tensor.matmul(ps[:, 7, 0:C], hhT[0:n, k % 2, j, :],
                                                w2s[0:n, bass.ds(e, 1), j, :],
                                                start=(j == 0), stop=(j == len(KB) - 1))
                    last.then_inc(s_dn, 1)

            turn_rows(0, 0)
            experts_of(0)
            for k in range(XB):
                step(0, k, hidden=k >= 1, down=k >= 2)
            with pe.Fori(1, NT // XB - 1) as i:
                experts_of(i)
                for k in range(XB):
                    step(i, k)
            experts_of(NT // XB - 1)
            for k in range(XB):
                step(NT // XB - 1, k, turn=k + 1 < XB)
            experts_of(NT // XB)
            step(NT // XB, 0, turn=False, up=False)
            step(NT // XB, 1, turn=False, up=False, hidden=False)


def kernel(**inputs):
    import concourse.bacc as bacc
    from concourse.bass_utils import run_bass_kernel_spmd

    a = {k: np.asarray(v) for k, v in inputs.items()}
    lin = a["L0_gnn_lin_W"]
    swapped = (np.arange(HD) + HD // 2) % HD
    wq, wk = a["L0_ffn_wq"], a["L0_ffn_wk"]
    wqr = wq.reshape(NH, HD, C)[:, swapped].reshape(NH * HD, C)
    wkr = wk.reshape(NKV, HD, C)[:, swapped].reshape(NKV * HD, C)
    inv_freq = 1.0 / 10000.0 ** (np.arange(0, HD, 2, dtype=np.float32) / HD)
    freqs = np.outer(np.arange(N, dtype=np.float32), inv_freq)
    emb = np.concatenate([freqs, freqs], axis=-1)
    sign = np.where(np.arange(HD) < HD // 2, -1, 1).astype(np.float32)
    cos = np.tile(np.cos(emb).T, (NH, 1)).astype(np.float32)
    sin = np.tile((np.sin(emb) * sign).T, (NH, 1)).astype(np.float32)
    later = np.where(np.arange(P)[:, None] > np.arange(P)[None, :], np.float32(-1e30), np.float32(0))
    lower = (np.arange(NE)[None, :] < np.arange(NE)[:, None]).astype(np.float32)
    row = np.arange(P)
    before = np.stack([row[:, None] < row[None, :], np.ones((P, P), bool)], axis=1).astype(np.float32)
    starts = np.arange(NR, dtype=np.float32) * REG
    token = np.arange(TILES)[None, None, :] * P + row[:, None, None]
    dest = (2 * token + np.arange(2)[None, :, None]).astype(np.int32)
    region = np.arange(NR)
    shared = [starts, (np.arange(NE)[None, :] < region[:, None]).ravel(), region % NE]
    tile_constants = np.concatenate(
        [np.broadcast_to(np.arange(N // P) * P, (P, N // P)), row[:, None], row[:, None] * P]
        + [np.broadcast_to(v, (P, v.size)) for v in shared], axis=1).astype(np.float32)
    pad = np.zeros((2 * NE, P, ROW), np.float32)
    pad.view(np.int32)[:, :, C + 1] = 2 * N + P * np.arange(2 * NE)[:, None] + row
    arrays = {
        "x": a["x"].reshape(TILES, P, C).transpose(1, 0, 2),
        "adj_t": a["adj"].reshape(NCH, CH, NGRP, GRP, P).transpose(0, 2, 4, 3, 1),
        "neigh_w": a["L0_gnn_neigh_W"],
        "lin1_t": lin[:, :C].T,
        "lin2_t": lin[:, C:].T,
        "ln1": a["L0_ffn_ln1_w"].reshape(C, 1),
        "ln2": a["L0_ffn_ln2_w"].reshape(C, 1),
        "wq_t": wq.T,
        "wqr_t": wqr.T,
        "wk_t": np.concatenate([wk.T, wkr.T], axis=1),
        "wv_t": a["L0_ffn_wv"].T,
        "wo_t": a["L0_ffn_wo"].T,
        "router_t": a["L0_ffn_router_w"].T,
        "tri_in": np.broadcast_to(lower, (P, NE, NE)),
        "w13_t": np.concatenate([a["L0_ffn_w1"].transpose(2, 0, 1), a["L0_ffn_w3"].transpose(2, 0, 1)], axis=2),
        "w2_t": a["L0_ffn_w2"].transpose(0, 2, 1),
        "cos_t": cos,
        "sin_t": sin,
        "ident_in": np.eye(P, dtype=np.float32),
        "mask_in": np.stack([later.T, later], axis=1),
        "before_in": before,
        "base_in": np.broadcast_to(starts[:NE], (P, NE)),
        "dest_in": dest,
        "tile_in": tile_constants,
        "pad_in": pad,
    }
    arrays = {k: np.ascontiguousarray(v) for k, v in arrays.items()}
    nc = bacc.Bacc("TRN2", target_bir_lowering=False, num_devices=1)
    args = [nc.dram_tensor(k, v.shape, mybir.dt.from_np(v.dtype), kind="ExternalInput").ap()
            for k, v in arrays.items()]
    out = nc.dram_tensor("out", (P, TILES, C), fp32, kind="ExternalOutput").ap()
    build(nc, *args, out)
    got = run_bass_kernel_spmd(nc, [arrays], core_ids=[0]).results[0]["out"]
    return np.ascontiguousarray(got.transpose(1, 0, 2)).reshape(N, C)
```
